# Optimizing a Trainium2 kernel written in Bass

```python
import numpy as np
import jax
import jax.numpy as jnp

def _softmax(x, axis=-1):
    return jax.nn.softmax(x, axis=axis)

def _gelu(x):
    return jax.nn.gelu(x, approximate=True)

def _silu(x):
    return jax.nn.silu(x)

def _sigmoid(x):
    return jax.nn.sigmoid(x)

def _layernorm(x, axis=-1, eps=1e-05):
    m = jnp.mean(x, axis=axis, keepdims=True)
    v = jnp.var(x, axis=axis, keepdims=True)
    return (x - m) / jnp.sqrt(v + eps)

def _scatter_add(tgt, idx, src, axis=0):
    return tgt.at[idx].add(src)

def _segment_sum(src, seg, n):
    return jax.ops.segment_sum(src, seg, n)
kernel_name = 'mk_adaln_ffn_d2_seqx_r4_22bd80'

def setup_inputs(seed: int=0):
    np.random.seed(seed)
    _w = jnp.asarray

    def _rec_inputs():
        import jax
        import jax.numpy as jnp
        _rk = jax.random.key(seed)
        x = -7.109e-05 + 0.9999 * jax.random.normal(jax.random.fold_in(_rk, 1), (32, 64, 1024), jnp.float32)
        _lenS = 64 - jax.random.randint(jax.random.fold_in(_rk, 7), (32,), 0, max(1, 64 // 4) + 1, jnp.int32)
        _lenS2 = 64 - jax.random.randint(jax.random.fold_in(_rk, 8), (32,), 0, max(1, 64 // 4) + 1, jnp.int32)
        itok_B_0_15 = jax.random.randint(jax.random.fold_in(_rk, 11), (32,), 0, 16, jnp.int32)
        itok_B_3_7 = jax.random.randint(jax.random.fold_in(_rk, 12), (32,), 3, 8, jnp.int32)
        return (x, itok_B_0_15, itok_B_3_7)
    x, itok_B_0_15, itok_B_3_7 = _rec_inputs()

    def _L0_cond_setup():
        import jax, jax.numpy as jnp
        import numpy as np
        NUM_CONDITIONS = 16
        IN_CH = 64
        OUT_CH = 64
        B = 64
        T = 1024
        key = jax.random.key(seed)
        k_x, k_w, k_c = jax.random.split(key, 3)
        x = jax.random.normal(k_x, (B, IN_CH, T), dtype=jnp.float32)
        bound = float(np.sqrt(6.0 / IN_CH))
        weights = jax.random.uniform(k_w, (NUM_CONDITIONS, IN_CH, OUT_CH), dtype=jnp.float32, minval=-bound, maxval=bound)
        condition = jax.random.randint(k_c, (B,), 0, NUM_CONDITIONS, dtype=jnp.int64)
        return {'x': x, 'weights': weights, 'condition': condition}
    _L0_cond_all = _L0_cond_setup()
    _L0_cond_in = {k: v for k, v in _L0_cond_all.items() if k in ('weights',)}
    del _L0_cond_all

    def _L0_ffn_setup():
        import jax, jax.numpy as jnp
        import numpy as np
        B_, S, D_IN, D_OUT = (4, 512, 1024, 1024)
        N, RANK, ALPHA = (8, 16, 32)
        SCALE = ALPHA / RANK
        key = jax.random.key(seed)
        kx, ka, kb, kw, kbias = jax.random.split(key, 5)
        x = jax.random.normal(kx, (B_, S, D_IN), dtype=jnp.float32)
        lora_A = jax.random.normal(ka, (N, RANK, D_IN), dtype=jnp.float32) * (1.0 / np.sqrt(D_IN))
        lora_B = jax.random.normal(kb, (N, D_OUT, RANK), dtype=jnp.float32) * (1.0 / np.sqrt(RANK))
        W = jax.random.normal(kw, (D_OUT, D_IN), dtype=jnp.float32) * (1.0 / np.sqrt(D_IN))
        bias = jax.random.normal(kbias, (D_OUT,), dtype=jnp.float32) * 0.01
        lora_weights = jnp.full((N,), 1.0 / N, dtype=jnp.float32)
        return {'x': x, 'lora_A': lora_A, 'lora_B': lora_B, 'W': W, 'bias': bias, 'lora_weights': lora_weights}
    _L0_ffn_all = _L0_ffn_setup()
    _L0_ffn_in = {k: v for k, v in _L0_ffn_all.items() if k in ('lora_A', 'lora_B', 'W', 'bias', 'lora_weights')}
    del _L0_ffn_all

    def _L1_cond_setup():
        import jax, jax.numpy as jnp
        import numpy as np
        RANK = 16
        ALPHA = 16.0
        SCALING = ALPHA / RANK
        N_ADAPTERS = 8
        IN_F = 1024
        OUT_F = 1024
        BATCH = 4
        SEQ = 512
        key = jax.random.key(seed)
        kx, ka, kb, ki = jax.random.split(key, 4)
        x = jax.random.normal(kx, (BATCH, SEQ, IN_F), dtype=jnp.float32)
        A = jax.random.normal(ka, (N_ADAPTERS, OUT_F, RANK), dtype=jnp.float32) * 0.02
        B = jax.random.normal(kb, (N_ADAPTERS, RANK, IN_F), dtype=jnp.float32) * 0.02
        adapter_ids = jax.random.randint(ki, (BATCH,), 0, N_ADAPTERS, dtype=jnp.int32)
        return {'x': x, 'A': A, 'B': B, 'adapter_ids': adapter_ids}
    _L1_cond_all = _L1_cond_setup()
    _L1_cond_in = {k: v for k, v in _L1_cond_all.items() if k in ('A', 'B')}
    del _L1_cond_all

    def _L1_ffn_setup():
        import jax, jax.numpy as jnp
        import numpy as np
        NF4 = jnp.array([-1.0, -0.6961928009986877, -0.5250730514526367, -0.39491748809814453, -0.28444138169288635, -0.18477343022823334, -0.09105003625154495, 0.0, 0.07958029955625534, 0.16093020141124725, 0.24611230194568634, 0.33791524171829224, 0.44070982933044434, 0.5626170039176941, 0.7229568362236023, 1.0], dtype=jnp.float32)
        BLOCK = 64

        def dequant_nf4(codes, scales):
            out_dim, in_dim = codes.shape
            vals = NF4[codes].reshape(out_dim, in_dim // BLOCK, BLOCK)
            return (vals * scales[:, :, None]).reshape(out_dim, in_dim)
        key = jax.random.key(seed)
        ks = jax.random.split(key, 7)
        H, I = (1024, 2752)
        B, S = (4, 512)
        return {'x': jax.random.normal(ks[0], (B, S, H), dtype=jnp.float32), 'gate_codes': jax.random.randint(ks[1], (I, H), 0, 16, dtype=jnp.int32), 'gate_scales': jax.random.uniform(ks[2], (I, H // BLOCK), dtype=jnp.float32) * 0.02, 'up_codes': jax.random.randint(ks[3], (I, H), 0, 16, dtype=jnp.int32), 'up_scales': jax.random.uniform(ks[4], (I, H // BLOCK), dtype=jnp.float32) * 0.02, 'down_codes': jax.random.randint(ks[5], (H, I), 0, 16, dtype=jnp.int32), 'down_scales': jax.random.uniform(ks[6], (H, I // BLOCK), dtype=jnp.float32) * 0.02}
    _L1_ffn_all = _L1_ffn_setup()
    _L1_ffn_in = {k: v for k, v in _L1_ffn_all.items() if k in ('gate_codes', 'gate_scales', 'up_codes', 'up_scales', 'down_codes', 'down_scales')}
    del _L1_ffn_all
    return {'x': x, 'itok_B_0_15': itok_B_0_15, 'itok_B_3_7': itok_B_3_7, 'L0_cond_weights': _L0_cond_in['weights'], 'L0_ffn_lora_A': _L0_ffn_in['lora_A'], 'L0_ffn_lora_B': _L0_ffn_in['lora_B'], 'L0_ffn_W': _L0_ffn_in['W'], 'L0_ffn_bias': _L0_ffn_in['bias'], 'L0_ffn_lora_weights': _L0_ffn_in['lora_weights'], 'L1_cond_A': _L1_cond_in['A'], 'L1_cond_B': _L1_cond_in['B'], 'L1_ffn_gate_codes': _L1_ffn_in['gate_codes'], 'L1_ffn_gate_scales': _L1_ffn_in['gate_scales'], 'L1_ffn_up_codes': _L1_ffn_in['up_codes'], 'L1_ffn_up_scales': _L1_ffn_in['up_scales'], 'L1_ffn_down_codes': _L1_ffn_in['down_codes'], 'L1_ffn_down_scales': _L1_ffn_in['down_scales']}

def reference(x, itok_B_0_15, itok_B_3_7, L0_cond_weights, L0_ffn_lora_A, L0_ffn_lora_B, L0_ffn_W, L0_ffn_bias, L0_ffn_lora_weights, L1_cond_A, L1_cond_B, L1_ffn_gate_codes, L1_ffn_gate_scales, L1_ffn_up_codes, L1_ffn_up_scales, L1_ffn_down_codes, L1_ffn_down_scales):
    import jax
    import jax.numpy as jnp

    def _L0_cond_ref(x, weights, condition):
        import jax, jax.numpy as jnp
        import numpy as np
        NUM_CONDITIONS = 16
        IN_CH = 64
        OUT_CH = 64
        B = 64
        T = 1024
        W = weights[condition]
        return jnp.einsum('bct,bcd->bdt', x, W)

    def _L0_ffn_ref(x, lora_A, lora_B, W, bias, lora_weights):
        import jax, jax.numpy as jnp
        import numpy as np
        B_, S, D_IN, D_OUT = (4, 512, 1024, 1024)
        N, RANK, ALPHA = (8, 16, 32)
        SCALE = ALPHA / RANK
        h = jnp.einsum('bsd,nrd->nbsr', x, lora_A)
        coef = (SCALE * lora_weights)[:, None, None]
        lora_out = jnp.einsum('nbsr,nor->bso', h, lora_B * coef)
        base = jnp.einsum('bsd,od->bso', x, W) + bias
        return base + lora_out

    def _L1_cond_ref(x, A, B, adapter_ids):
        import jax, jax.numpy as jnp
        import numpy as np
        RANK = 16
        ALPHA = 16.0
        SCALING = ALPHA / RANK
        N_ADAPTERS = 8
        IN_F = 1024
        OUT_F = 1024
        BATCH = 4
        SEQ = 512
        B_sel = B[adapter_ids]
        A_sel = A[adapter_ids]
        Bx = jnp.einsum('bni,bri->bnr', x, B_sel)
        out = jnp.einsum('bnr,bor->bno', Bx, A_sel)
        return out * SCALING

    def _L1_ffn_ref(x, gate_codes, gate_scales, up_codes, up_scales, down_codes, down_scales):
        import jax, jax.numpy as jnp
        import numpy as np
        NF4 = jnp.array([-1.0, -0.6961928009986877, -0.5250730514526367, -0.39491748809814453, -0.28444138169288635, -0.18477343022823334, -0.09105003625154495, 0.0, 0.07958029955625534, 0.16093020141124725, 0.24611230194568634, 0.33791524171829224, 0.44070982933044434, 0.5626170039176941, 0.7229568362236023, 1.0], dtype=jnp.float32)
        BLOCK = 64

        def dequant_nf4(codes, scales):
            out_dim, in_dim = codes.shape
            vals = NF4[codes].reshape(out_dim, in_dim // BLOCK, BLOCK)
            return (vals * scales[:, :, None]).reshape(out_dim, in_dim)
        Wg = dequant_nf4(gate_codes, gate_scales)
        Wu = dequant_nf4(up_codes, up_scales)
        Wd = dequant_nf4(down_codes, down_scales)
        gate = jnp.einsum('bsh,ih->bsi', x, Wg)
        up = jnp.einsum('bsh,ih->bsi', x, Wu)
        inter = jax.nn.silu(gate) * up
        return jnp.einsum('bsi,hi->bsh', inter, Wd)
    x = x + _L0_ffn_ref(_L0_cond_ref(x, L0_cond_weights, itok_B_0_15), L0_ffn_lora_A, L0_ffn_lora_B, L0_ffn_W, L0_ffn_bias, L0_ffn_lora_weights)
    x = x + _L1_ffn_ref(_L1_cond_ref(x, L1_cond_A, L1_cond_B, itok_B_3_7), L1_ffn_gate_codes, L1_ffn_gate_scales, L1_ffn_up_codes, L1_ffn_up_scales, L1_ffn_down_codes, L1_ffn_down_scales)
    return x

_drawn_inputs = setup_inputs


def setup_inputs(seed=0):
    import zlib

    import numpy as np

    out = dict(_drawn_inputs(seed))
    spreads = {'L0_ffn_lora_weights': (0.125, 0.2)}
    factors = {'L0_ffn_bias': 8.0,
     'L1_cond_A': 8.0,
     'L1_cond_B': 8.0,
     'L1_ffn_gate_scales': 8.0,
     'L1_ffn_up_scales': 8.0,
     'L1_ffn_down_scales': 8.0}
    for name, (base, spread) in spreads.items():
        noise = np.random.default_rng([zlib.crc32(name.encode()), seed]).standard_normal(out[name].shape)
        drawn = base * np.exp(spread * noise) if base else spread * noise
        out[name] = jnp.asarray(drawn.astype(out[name].dtype))
    for name, factor in factors.items():
        out[name] = (out[name] * factor).astype(out[name].dtype)
    return out
```

```python
from contextlib import ExitStack

import numpy as np

import concourse.bass as bass
from concourse import mybir

F32 = mybir.dt.float32
F32R = mybir.dt.float32r
I32 = mybir.dt.int32
ALU = mybir.AluOpType
ACT = mybir.ActivationFunctionType
ds = bass.ds

NF4 = [-1.0, -0.6961928009986877, -0.5250730514526367, -0.39491748809814453, -0.28444138169288635,
       -0.18477343022833234, -0.09105003625154495, 0.0, 0.07958029955625534, 0.16093020141124725,
       0.24611230194568634, 0.33791524171829224, 0.44070982933044434, 0.5626170039176941,
       0.7229568362236023, 1.0]
MID = 8
UPPER = [(0.08134990185499191, 0.07958029955625534), (0.0918029248714447, 0.06250645220279694),
         (0.12190713733434677, -0.046918708831071854), (0.2770431339740753, -0.9393019676208496)]
LOWER = [(0.09105003625154495, 0.09105003625154495), (0.09966794401407242, 0.11423040181398392),
         (0.1301555186510086, 0.2558600902557373), (0.30380719900131226, 1.430457592010498)]
LINES = [UPPER[0], UPPER[1], LOWER[0], LOWER[1], UPPER[2], LOWER[2], UPPER[3], LOWER[3]]
NLINES = len(LINES)
COMBOS = 7


def check_lines():
    for code, level in enumerate(NF4):
        at = [np.float32(np.float64(code - MID) * m + c) for m, c in UPPER + LOWER]
        up, low = max(0.0, *at[:4]), min(0.0, *at[4:])
        assert np.float32(up + low) == np.float32(level)


def adaln_ffn(nc, x, cond_id, adapter_id, cond_w, lora_a, lora_b, w0, bias0, lora_w, ad_a, ad_b,
              gate_codes, gate_scales, up_codes, up_scales, down_codes, down_scales, out):
    check_lines()
    SAMPLES, CH, D = x.shape
    P = 128
    ROWS = SAMPLES * CH
    NT = ROWS // P
    PER = P // CH
    DC = D // P
    HALF = 512
    NCOND = cond_w.shape[0]
    NAD, RANK, _ = ad_b.shape
    NR = NAD * RANK
    LORA_SCALE = 32 / lora_a.shape[1]
    HID = gate_codes.shape[0]
    BLK = D // gate_scales.shape[1]
    SB = gate_scales.shape[1]
    DSB = down_scales.shape[1]
    CHUNKS = HID // P
    REM = HID - CHUNKS * P
    G = 3
    GROUPS = CHUNKS // G
    NB = ROWS // HALF
    TPB = HALF // P
    ITER_A = 7
    UPI = 2 * CHUNKS // ITER_A
    TAIL_U = 2 * CHUNKS
    REST_U = TAIL_U + 1
    DOWN_U = REST_U + 1
    UNITS = DOWN_U + CHUNKS
    assert NR == P and 2 * REM == P and GROUPS * G == CHUNKS and ITER_A * UPI == TAIL_U
    assert UPI == 6 and NT == 2 * ITER_A + 2 and GROUPS % 2 == 1 and BLK == 64 and RANK == 16
    RING = 4

    x_rows = x.rearrange("s c d -> (s c) d")
    out_rows = out.rearrange("s c d -> (s c) d")
    x1_dram = nc.dram_tensor("x1_scratch", [ROWS, D], F32, kind="Internal").ap()
    ga_hi_dram = nc.dram_tensor("ga_hi_scratch", [CHUNKS + 1, P, 2 * P], F32, kind="Internal").ap()
    ga_lo_dram = nc.dram_tensor("ga_lo_scratch", [CHUNKS + 1, P, 2 * P], F32, kind="Internal").ap()

    with ExitStack() as ctx:
        def sb(name, shape, dt, where=ctx):
            return where.enter_context(nc.sbuf_tensor(name, shape, dt))

        def sem(name):
            return ctx.enter_context(nc.semaphore(name))

        ident = sb("ident", [P, P], F32)
        mid = sb("mid", [P, 1], I32)
        one = sb("one", [P, 1], F32)
        line_c = sb("line_c", [P, NLINES], F32)
        gu_scales = sb("gu_scales", [P, CHUNKS + 1, 2, SB], F32)
        d_scales = sb("d_scales", [P, DC, DSB], F32)
        mask = sb("mask", [P, SAMPLES], F32)
        bx_hi = sb("bx_hi", [P, ROWS], F32R)
        bx_lo = sb("bx_lo", [P, ROWS], F32R)
        codes = sb("codes", [P, 2, D], I32)
        ring = sb("ring", [P, RING, D], F32)
        lower = sb("lower", [P, D], F32)
        val = sb("val", [P, 2, D], F32)

        phase_a = ExitStack()
        we_hi = sb("we_hi", [P, DC, D], F32R, phase_a)
        we_lo = sb("we_lo", [P, DC, D], F32R, phase_a)
        xs = sb("xs", [P, 2, D], F32, phase_a)
        x1s = sb("x1s", [P, D], F32, phase_a)
        x1t = sb("x1t", [P, DC, P], F32, phase_a)
        y_hi = sb("y_hi", [P, DC, P], F32R, phase_a)
        y_lo = sb("y_lo", [P, DC, P], F32R, phase_a)
        cond_bd = sb("cond_bd", [P, NT, P], F32, phase_a)
        ad_bt = sb("ad_bt", [P, DC, P], F32, phase_a)
        ad_at = sb("ad_at", [P, DC, NAD, RANK], F32, phase_a)
        wt = sb("wt", [P, 2, DC, P], F32, phase_a)
        bias_b = sb("bias_b", [P, D], F32, phase_a)
        ga_f = sb("ga_f", [P, 2 * P], F32, phase_a)
        ga_hi = sb("ga_hi", [P, 2 * P], F32R, phase_a)
        ga_lo = sb("ga_lo", [P, 2 * P], F32R, phase_a)
        bx_f = sb("bx_f", [P, P], F32, phase_a)
        la = sb("la", [P, D], F32, phase_a)
        lb = sb("lb", [P, NAD, DC, RANK], F32, phase_a)
        lbt = sb("lbt", [P, D], F32, phase_a)
        ad_braw = sb("ad_braw", [P, D], F32, phase_a)
        lw = sb("lw", [P, NAD], F32, phase_a)
        cond_ids = sb("cond_ids", [1, SAMPLES], I32, phase_a)
        ad_ids = sb("ad_ids", [P, SAMPLES], I32, phase_a)
        part_i = sb("part_i", [P, 1], I32, phase_a)
        part_ad = sb("part_ad", [P, 1], I32, phase_a)
        part_f = sb("part_f", [P, 1], F32, phase_a)
        ad_araw = ring[:, 1, :].rearrange("p (n q r) -> p n q r", n=NAD, q=DC)
        lbq = ring[:, 0, :].rearrange("p (q n r) -> p q n r", n=NAD, q=DC)
        w_chunk = [x1s[:, :].rearrange("p (q j) -> p q j", q=DC), x1t[:, :, :]]
        phase_a.close()

        acc = sb("acc", [P, NT, D], F32)
        wd_hi = sb("wd_hi", [P, 2, G, D], F32R)
        wd_lo = sb("wd_lo", [P, 2, G, D], F32R)
        in_hi = sb("in_hi", [P, 2, G, HALF], F32R)
        in_lo = sb("in_lo", [P, 2, G, HALF], F32R)
        st_hi = sb("st_hi", [P, G, 2, P], F32R)
        st_lo = sb("st_lo", [P, G, 2, P], F32R)
        silu_g = sb("silu_g", [P, 2, HALF], F32)
        inter = sb("inter", [P, 2, HALF], F32)

        ps_y = ctx.enter_context(nc.psum_tensor("ps_y", [P, D], F32))
        ps_z = ctx.enter_context(nc.psum_tensor("ps_z", [P, D], F32))
        ps_t = ctx.enter_context(nc.psum_tensor("ps_t", [P, D], F32))
        ps_g = ctx.enter_context(nc.psum_tensor("ps_g", [P, HALF], F32))
        ps_u = ctx.enter_context(nc.psum_tensor("ps_u", [P, HALF], F32))
        ps_o = [ps_y, ps_z]

        ids_in = sem("ids_in")
        ad_ids_in = sem("ad_ids_in")
        lora_in = sem("lora_in")
        ad_b_in = sem("ad_b_in")
        ad_a_in = sem("ad_a_in")
        bias_in = sem("bias_in")
        scales_in = sem("scales_in")
        bd_in = sem("bd_in")
        w_in = [sem(f"w_in{k}") for k in range(2)]
        x_in = [sem(f"x_in{k}") for k in range(2)]
        codes_in = [sem(f"codes_in{k}") for k in range(2)]
        stage_in = [sem(f"stage_in{k}") for k in range(G)]
        acc_in = [sem(f"acc_in{k}") for k in range(NB)]
        x1_out = sem("x1_out")
        ga_out = sem("ga_out")
        out_done = sem("out_done")
        consts_ready = sem("consts_ready")
        ident_ready = sem("ident_ready")
        bd_zeroed = sem("bd_zeroed")
        line_c_ready = sem("line_c_ready")
        part_ready = sem("part_ready")
        mask_step = sem("mask_step")
        lw_ready = sem("lw_ready")
        ad_at_ready = sem("ad_at_ready")
        lb_scaled = sem("lb_scaled")
        setup_t = sem("setup_t")
        setup_evac = sem("setup_evac")
        we_mm = sem("we_mm")
        we_hi_ready = sem("we_hi_ready")
        we_lo_ready = sem("we_lo_ready")
        shifted = sem("shifted")
        lines = sem("lines")
        combo = sem("combo")
        scaled = sem("scaled")
        t_done = sem("t_done")
        wt_ready = sem("wt_ready")
        ga_mm = sem("ga_mm")
        ga_evac = sem("ga_evac")
        ga_step = sem("ga_step")
        ga_split = sem("ga_split")
        y_mm = sem("y_mm")
        y_hi_ready = sem("y_hi_ready")
        y_lo_ready = sem("y_lo_ready")
        z_mm = sem("z_mm")
        xb_ready = sem("xb_ready")
        x1_ready = sem("x1_ready")
        x1t_mm = sem("x1t_mm")
        x1t_ready = sem("x1t_ready")
        bx_mm = sem("bx_mm")
        bx_masked = sem("bx_masked")
        bx_step = sem("bx_step")
        bx_split = sem("bx_split")
        wd_hi_ready = sem("wd_hi_ready")
        wd_lo_ready = sem("wd_lo_ready")
        gu_mm = sem("gu_mm")
        silu_ready = sem("silu_ready")
        inter_ready = sem("inter_ready")
        in_hi_ready = sem("in_hi_ready")
        in_lo_ready = sem("in_lo_ready")
        down_mm = sem("down_mm")
        added = sem("added")

        REST = -1

        def loads_of(pair, par, behind_tail=False):
            return 16 * (pair + 1 + (behind_tail and par == 0))

        def chunk_no(g, b, k):
            return b if is_rest(g) else NB * (1 + G * g) + G * b + k

        def is_rest(g):
            return isinstance(g, int) and g == REST

        def next_chunk(g, b, k, last):
            if k < 0 or k >= G or (b == NB - 1 and last):
                return None
            if b == NB - 1:
                return (0 if is_rest(g) else g + 1), 0, k
            return (g, b + 1, k) if k == 0 or not is_rest(g) else None

        def chunk_slot(g, b, k):
            return b % 2 if is_rest(g) else (G * b + k) % 2

        def next_units(g):
            return DOWN_U if is_rest(g) else DOWN_U + G * (g + 1)

        def wait(eng, semaphore, count):
            if not isinstance(count, int) or count > 0:
                eng.wait_ge(semaphore, count)

        block = ctx.enter_context(nc.Block())

        @block.sync
        def _(sp):
            def load_x(tile, slot):
                if not isinstance(tile, int) or tile > 1:
                    sp.wait_ge(y_mm, tile - 1)
                    sp.wait_ge(xb_ready, tile - 1)
                sp.dma_start(xs[:, slot, :], x_rows[ds(tile * P, P), :]).then_inc(x_in[slot], 16)

            def load_gu(n, par, chunk):
                wait(sp, lines, NLINES * (n - 1))
                sp.dma_start(codes[:, par, :], (up_codes if par else gate_codes)[ds(chunk * P, P), :]
                             ).then_inc(codes_in[par], 16)

            def load_down(n, par, col, width):
                sp.wait_ge(lines, NLINES * (n - 1))
                sp.dma_start(codes[:, par, :].rearrange("p (t i) -> p t i", t=DC)[:, :, 0:width],
                             down_codes.rearrange("(t p) i -> p t i", p=P)[:, :, ds(col, width)]
                             ).then_inc(codes_in[par], 16)

            def store_x1(tile):
                sp.wait_ge(x1_ready, tile + 1)
                sp.dma_start(x1_dram[ds(tile * P, P), :], x1s[:, :]).then_inc(x1_out, 16)

            def store_ga(chunk):
                sp.wait_ge(ga_split, chunk + 1)
                for src, dst in ((ga_hi, ga_hi_dram), (ga_lo, ga_lo_dram)):
                    sp.dma_start(dst[ds(chunk, 1), :, :].rearrange("a p n -> p a n"),
                                 src[:, :].bitcast(F32).rearrange("p (a n) -> p a n", a=1)
                                 ).then_inc(ga_out, 16)

            load_gu(0, 0, 0)
            sp.dma_start(cond_ids[:, :], cond_id.rearrange("(a s) -> a s", a=1)).then_inc(ids_in, 16)
            load_x(0, 0)
            load_x(1, 1)
            load_gu(1, 1, 0)
            sp.wait_ge(ids_in, 16)
            sp.wait_ge(bd_zeroed, 1)
            with sp.Fori(0, NT) as m:
                for half in range(PER):
                    cid = sp.value_load(cond_ids[0:1, ds(PER * m + half, 1)], min_val=0, max_val=NCOND - 1)
                    sp.dma_start(cond_bd[half * CH:(half + 1) * CH, ds(m, 1), half * CH:(half + 1) * CH],
                                 cond_w[ds(cid, 1), :, :].rearrange("a c e -> c a e")).then_inc(bd_in, 16)

            def iteration(i, last):
                for s in range(UPI):
                    n = UPI * i + s + 2
                    if not last or s < UPI - 2:
                        load_gu(n, s % 2, G * i + s // 2 + 1)
                    elif s == UPI - 2:
                        sp.wait_ge(lines, NLINES * (n - 1))
                        for half, src in enumerate((gate_codes, up_codes)):
                            sp.dma_start(codes[half * REM:(half + 1) * REM, 0, :], src[CHUNKS * P:HID, :]
                                         ).then_inc(codes_in[0], 16)
                    else:
                        load_down(n, 1, CHUNKS * P, REM)
                    if s == 1:
                        store_x1(2 * i)
                    if s == 2:
                        load_x(2 * i + 2, 0)
                        store_ga(G * i)
                    if s == 4:
                        store_ga(G * i + 1)
                        store_x1(2 * i + 1)
                    if s == 5:
                        load_x(2 * i + 3, 1)
                        store_ga(G * i + 2)

            with sp.Fori(0, ITER_A - 1) as i:
                iteration(i, False)
            iteration(ITER_A - 1, True)

            load_down(DOWN_U, 0, 0, P)
            store_x1(NT - 2)
            store_ga(CHUNKS)
            load_down(DOWN_U + 1, 1, P, P)
            store_x1(NT - 1)
            sp.wait_ge(z_mm, NT)
            sp.wait_ge(x1_out, 16 * NT)
            for b in range(NB):
                sp.dma_start(acc[:, b * TPB:(b + 1) * TPB, :],
                             x1_dram[b * HALF:(b + 1) * HALF, :].rearrange("(t p) d -> p t d", p=P)
                             ).then_inc(acc_in[b], 16)
            with sp.Fori(1, CHUNKS // 2) as j:
                for par in range(2):
                    load_down(DOWN_U + 2 * j + par, par, (2 * j + par) * P, P)
            load_down(DOWN_U + CHUNKS - 1, 0, (CHUNKS - 1) * P, P)
            for t in range(NT):
                sp.wait_ge(added, NT * GROUPS + t + 1)
                sp.dma_start(out_rows[t * P:(t + 1) * P, :], acc[:, t, :]).then_inc(out_done, 16)
            sp.wait_ge(out_done, 16 * NT)

        @block.gpsimd
        def _(pool):
            pool.memset(ident[:, :], 0.0).then_inc(ident_ready, 1)
            pool.wait_ge(ident_ready, 1)
            pool.affine_select(out=ident[:, :], in_=ident[:, :], compare_op=ALU.not_equal, fill=1.0, base=0,
                               pattern=[[-1, P]], channel_multiplier=1).then_inc(ident_ready, 1)
            pool.iota(part_i[:, :], pattern=[[0, 1]], base=0, channel_multiplier=1).then_inc(part_ready, 1)

            def shift(pair, par, behind_tail=False):
                pool.wait_ge(codes_in[par], loads_of(pair, par, behind_tail))
                pool.tensor_tensor(codes[:, par, :], codes[:, par, :], mid[:, :].to_broadcast([P, D]), ALU.subtract
                                   ).then_inc(shifted, 1)

            def scale(n, par, scales, part=None):
                pool.wait_ge(combo, COMBOS * (n + 1))
                v = val[:, par, :].rearrange("p (b j) -> p b j", j=BLK) if part is None else part
                pool.tensor_tensor(v, v, scales, ALU.mult).then_inc(scaled, 1)

            def gu_scale(chunk, kind):
                return gu_scales[:, ds(chunk, 1), kind, :].rearrange("p a b -> p (a b)").unsqueeze(2
                                 ).to_broadcast([P, SB, BLK])

            def add_bias(tile, slot, i):
                pool.wait_ge(x_in[slot], 16 * (i + 1))
                wait(pool, x1_out, 16 * tile)
                wait(pool, x1t_mm, tile)
                pool.tensor_tensor(x1s[:, :], xs[:, slot, :], bias_b[:, :], ALU.add).then_inc(xb_ready, 1)

            def split_ga(chunk):
                pool.wait_ge(ga_evac, chunk + 1)
                wait(pool, ga_out, 32 * chunk)
                pool.tensor_tensor(ga_hi[:, :], ga_f[:, :], one[:, :].to_broadcast([P, 2 * P]), ALU.mult
                                   ).then_inc(ga_step, 1)
                pool.wait_ge(ga_step, chunk + 1)
                pool.tensor_tensor(ga_lo[:, :], ga_f[:, :], ga_hi[:, :].bitcast(F32), ALU.subtract
                                   ).then_inc(ga_split, 1)

            def split_bx(tile):
                hi, lo = bx_hi[:, ds(tile * P, P)], bx_lo[:, ds(tile * P, P)]
                pool.wait_ge(bx_masked, tile + 1)
                pool.tensor_tensor(hi, bx_f[:, :], one[:, :].to_broadcast([P, P]), ALU.mult
                                   ).then_inc(bx_step, 1)
                pool.wait_ge(bx_step, tile + 1)
                pool.tensor_tensor(lo, bx_f[:, :], hi.bitcast(F32), ALU.subtract).then_inc(bx_split, 1)

            def iteration(i, last):
                for s in range(UPI):
                    n, par = UPI * i + s, s % 2
                    if s == 0:
                        add_bias(2 * i, 0, i)
                    if s == 3:
                        add_bias(2 * i + 1, 1, i)
                    shift(UPI // 2 * i + s // 2 + 1, par, last and s >= UPI - 2)
                    scale(n, par, gu_scale(G * i + s // 2, par))
                    if s == 2:
                        split_ga(G * i)
                        split_bx(2 * i)
                    if s == 4:
                        split_ga(G * i + 1)
                    if s == 5:
                        split_ga(G * i + 2)
                        split_bx(2 * i + 1)

            pool.memset(mid[:, :], MID).then_inc(consts_ready, 1)
            pool.memset(one[:, :], 1.0).then_inc(consts_ready, 1)
            pool.wait_ge(consts_ready, 2)
            shift(0, 0)
            shift(0, 1)
            pool.wait_ge(bias_in, 16)
            pool.wait_ge(scales_in, 16 * 5)
            pool.wait_ge(we_mm, DC)
            iteration(0, False)
            with pool.Fori(1, ITER_A - 1) as i:
                iteration(i, False)
            iteration(ITER_A - 1, True)

            def scale_down(c, n, par):
                v = val[:, par, :].rearrange("p (t b j) -> p t b j", t=DC, j=BLK)
                scale(n, par, d_scales[:, :, ds(2 * c, 2)].unsqueeze(3).to_broadcast([P, DC, 2, BLK]), v)

            add_bias(NT - 2, 0, ITER_A)
            scale(TAIL_U, 0, gu_scale(CHUNKS, 0))
            shift(DOWN_U // 2, 0, True)
            v = val[:, 1, :].rearrange("p (t j) -> p t j", t=DC)[:, :, 0:REM]
            scale(REST_U, 1, d_scales[:, :, DSB - 1:DSB].to_broadcast([P, DC, BLK]), v)
            split_ga(CHUNKS)
            split_bx(NT - 2)
            add_bias(NT - 1, 1, ITER_A)
            shift(DOWN_U // 2, 1, True)
            split_bx(NT - 1)
            with pool.Fori(0, (CHUNKS - 3) // 2) as j:
                for par in range(2):
                    c = 2 * j + par
                    shift(DOWN_U // 2 + j + 1, par, True)
                    scale_down(c, DOWN_U + c, par)
            for c in range(CHUNKS - 3, CHUNKS):
                if c + 2 < CHUNKS:
                    shift((DOWN_U + c) // 2 + 1, c % 2, True)
                scale_down(c, DOWN_U + c, c % 2)

        @block.scalar
        def _(act):
            act.dma_start(lb[:, :, :, :].rearrange("p n q r -> p n (q r)"),
                          lora_b.rearrange("n (p q) r -> p n (q r)", p=P)).then_inc(lora_in, 16)
            act.dma_start(lw[:, :], lora_w.partition_broadcast(P)).then_inc(lora_in, 16)
            act.dma_start(la[:, :], lora_a.rearrange("n r d -> (n r) d")).then_inc(lora_in, 16)
            w_qj = w0.rearrange("(p q) j -> p q j", p=P)

            def load_w(jc):
                if jc >= 2:
                    act.wait_ge(we_mm, jc - 1)
                act.dma_start(w_chunk[jc % 2], w_qj[:, :, jc * P:(jc + 1) * P]).then_inc(w_in[jc % 2], 16)

            load_w(0)
            load_w(1)
            act.dma_start(ad_araw.rearrange("p n q r -> p n (q r)"),
                          ad_a.rearrange("n (p q) r -> p n (q r)", p=P)).then_inc(ad_a_in, 16)
            act.dma_start(ad_braw[:, :], ad_b.rearrange("n r d -> (n r) d")).then_inc(ad_b_in, 16)
            act.dma_start(ad_ids[:, :], adapter_id.partition_broadcast(P)).then_inc(ad_ids_in, 16)
            act.dma_start(bias_b[:, :], bias0.partition_broadcast(P)).then_inc(bias_in, 16)
            for kind, src in enumerate((gate_scales, up_scales)):
                act.dma_start(gu_scales[:, 0:CHUNKS, kind, :],
                              src[0:CHUNKS * P, :].rearrange("(c p) b -> p c b", p=P)).then_inc(scales_in, 16)
                act.dma_start(gu_scales[kind * REM:(kind + 1) * REM, CHUNKS, 0, :], src[CHUNKS * P:HID, :]
                              ).then_inc(scales_in, 16)
            act.dma_start(d_scales[:, :, :], down_scales.rearrange("(t p) b -> p t b", p=P)
                          ).then_inc(scales_in, 16)

            def line(n, k, par):
                if k == 0:
                    act.wait_ge(shifted, n + 1)
                if k < RING:
                    wait(act, combo, COMBOS * n - 4 + k)
                elif k % 2 == 0:
                    act.wait_ge(combo, COMBOS * n + k // 2 - 1)
                slope, _ = LINES[k]
                act.activation(ring[:, k % RING, :], codes[:, par, :], ACT.Relu if k == 0 else ACT.Identity,
                               bias=line_c[:, k:k + 1], scale=slope).then_inc(lines, 1)

            def first_lines(n, par):
                for k in range(RING):
                    line(n, k, par)

            def last_lines(n, par):
                for k in range(RING, NLINES):
                    line(n, k, par)

            def evac_t(n, par):
                act.wait_ge(t_done, n + 1)
                wait(act, ga_mm, n - 1)
                act.activation(wt[:, par, :, :], ps_t[:, :].rearrange("p (q i) -> p q i", q=DC), ACT.Copy
                               ).then_inc(wt_ready, 1)

            def evac_y(tile):
                act.wait_ge(y_mm, tile + 1)
                wait(act, z_mm, tile)
                act.activation(y_hi[:, :, :].rearrange("p q t -> p (q t)"), ps_y[:, :], ACT.Copy
                               ).then_inc(y_hi_ready, 1)

            def evac_x1t(tile):
                act.wait_ge(x1t_mm, tile + 1)
                wait(act, bx_mm, tile)
                act.activation(x1t[:, :, :].rearrange("p q t -> p (q t)"), ps_y[:, :], ACT.Copy
                               ).then_inc(x1t_ready, 1)

            def evac_ga(chunk):
                act.wait_ge(ga_mm, 2 * chunk + 2)
                wait(act, ga_split, chunk)
                act.activation(ga_f[:, :], ps_g[:, 0:2 * P], ACT.Copy).then_inc(ga_evac, 1)

            act.wait_ge(setup_t, 1)
            act.activation(lbt[:, :], ps_t[:, :], ACT.Copy).then_inc(setup_evac, 1)
            act.wait_ge(setup_t, 2)
            act.activation(ad_bt[:, :, :].rearrange("p q t -> p (q t)"), ps_y[:, :], ACT.Copy
                           ).then_inc(setup_evac, 1)
            act.wait_ge(line_c_ready, NLINES)
            act.wait_ge(ad_at_ready, 1)
            for jc in range(DC):
                if jc < RING:
                    line(0, jc, 0)
                if jc + 2 < DC:
                    load_w(jc + 2)
                act.wait_ge(we_mm, jc + 1)
                act.activation(we_hi[:, jc, :].rearrange("j (p q) -> j q p", q=DC),
                               ps_o[1 - jc % 2][:, :].rearrange("j (q p) -> j q p", q=DC), ACT.Copy
                               ).then_inc(we_hi_ready, 1)
            evac_y(0)
            last_lines(0, 0)

            def iteration(i):
                a, b = 2 * i, 2 * i + 1
                for s in range(UPI):
                    n, par = UPI * i + s, s % 2
                    if s == 2:
                        evac_x1t(a)
                        evac_ga(G * i)
                    if s == 5:
                        evac_x1t(b)
                    first_lines(n + 1, 1 - par)
                    if s == 2:
                        evac_y(b)
                    if s == 4:
                        evac_ga(G * i + 1)
                    evac_t(n, par)
                    if s == 5:
                        evac_y(a + 2)
                    last_lines(n + 1, 1 - par)
                evac_ga(G * i + 2)

            iteration(0)
            with act.Fori(1, ITER_A) as i:
                iteration(i)

            first_lines(REST_U, 1)
            evac_t(TAIL_U, 0)
            last_lines(REST_U, 1)
            evac_x1t(NT - 2)
            act.wait_ge(ga_mm, TAIL_U + 1)
            act.wait_ge(ga_split, CHUNKS)
            act.activation(ga_f[:, 0:P], ps_g[:, 0:P], ACT.Copy)
            act.activation(ga_f[:, P:P + REM], ps_g[:, REM:P], ACT.Copy)
            act.activation(ga_f[:, P + REM:2 * P], ps_g[:, 0:REM], ACT.Copy).then_inc(ga_evac, 1)
            evac_y(NT - 1)
            evac_x1t(NT - 1)

            def stage(g, k):
                chunk = CHUNKS if is_rest(g) else G * g + k
                for dst, src in ((st_hi, ga_hi_dram), (st_lo, ga_lo_dram)):
                    act.dma_start(dst[:, k:k + 1, :, :].bitcast(F32).rearrange("p a m i -> p a (m i)"),
                                  src[ds(chunk, 1), :, :].rearrange("a p n -> p a n")).then_inc(stage_in[k], 16)

            def silu(g, b, k):
                q, rows = chunk_no(g, b, k), REM if is_rest(g) else P
                act.wait_ge(gu_mm, q + 1)
                wait(act, inter_ready, q - 1)
                act.activation(silu_g[0:rows, chunk_slot(g, b, k), :], ps_g[0:rows, :], ACT.Silu
                               ).then_inc(silu_ready, 1)

            def inter_hi(g, b, k):
                q, rows = chunk_no(g, b, k), REM if is_rest(g) else P
                act.wait_ge(inter_ready, q + 1)
                act.activation(in_hi[0:rows, b % 2, k, :], inter[0:rows, chunk_slot(g, b, k), :], ACT.Copy
                               ).then_inc(in_hi_ready, 1)

            def evac_wd(n, gpar, k):
                act.wait_ge(t_done, n + 1)
                act.activation(wd_hi[:, gpar, k, :], ps_t[:, :], ACT.Copy).then_inc(wd_hi_ready, 1)

            def group(g, gpar, last=False):
                n0, npar = next_units(g), 1 - gpar
                for b in range(NB):
                    for s in range(TPB):
                        if b == 0 and s == 0 and not last:
                            first_lines(n0, npar)
                        work = next_chunk(g, b, s - 1, last)
                        if work:
                            silu(*work)
                            if b == NB - 2 and not last:
                                stage(0 if is_rest(g) else g + 1, s - 1)
                        if b < G and s < 2 and not last:
                            line(n0 + b, RING + 2 * s, (npar + b) % 2)
                            line(n0 + b, RING + 2 * s + 1, (npar + b) % 2)
                        if work:
                            inter_hi(*work)
                    if b > 0 and not last:
                        evac_wd(n0 + b - 1, npar, b - 1)
                    if b < G - 1 and not last:
                        first_lines(n0 + b + 1, (npar + b + 1) % 2)

            act.wait_ge(ga_out, 32 * (CHUNKS + 1))
            act.wait_ge(bx_split, NT)
            act.wait_ge(x1_out, 16 * NT)
            stage(REST, 0)
            for k in range(1, G):
                stage(0, k)
            evac_wd(REST_U, 1, 0)
            silu(REST, 0, 0)
            inter_hi(REST, 0, 0)
            group(REST, 1)
            with act.Fori(0, GROUPS // 2) as j:
                group(2 * j, 0)
                group(2 * j + 1, 1)
            group(GROUPS - 1, 0, last=True)

        @block.vector
        def _(dve):
            for k, (_, at_mid) in enumerate(LINES):
                dve.memset(line_c[:, k:k + 1], at_mid).then_inc(line_c_ready, 1)
            dve.memset(cond_bd[:, :, :], 0.0).then_inc(bd_zeroed, 1)
            dve.wait_ge(lora_in, 16 * 3)
            dve.tensor_scalar(lw[:, :], lw[:, :], LORA_SCALE, None, ALU.mult).then_inc(lw_ready, 1)
            dve.wait_ge(lw_ready, 1)
            lb_n = lb[:, :, :, :].rearrange("p n q r -> p n (q r)")
            dve.tensor_tensor(lb_n, lb_n, lw[:, :].unsqueeze(2).to_broadcast([P, NAD, P]), ALU.mult
                              ).then_inc(lw_ready, 1)
            dve.wait_ge(lw_ready, 2)
            dve.tensor_copy(lbq, lb[:, :, :, :].rearrange("p n q r -> p q n r")).then_inc(lb_scaled, 1)
            dve.wait_ge(ad_a_in, 16)
            dve.tensor_copy(ad_at[:, :, :, :], ad_araw.rearrange("p n q r -> p q n r")).then_inc(ad_at_ready, 1)
            dve.wait_ge(part_ready, 1)
            dve.tensor_scalar(part_ad[:, :], part_i[:, :], RANK.bit_length() - 1, None, ALU.logical_shift_right
                              ).then_inc(mask_step, 1)
            dve.wait_ge(mask_step, 1)
            dve.tensor_copy(part_f[:, :], part_ad[:, :]).then_inc(mask_step, 1)
            dve.wait_ge(mask_step, 2)
            dve.wait_ge(ad_ids_in, 16)
            dve.tensor_scalar(mask[:, :], ad_ids[:, :], part_f[:, 0:1], None, ALU.is_equal
                              ).then_inc(mask_step, 1)
            for jc in range(DC):
                dve.wait_ge(we_hi_ready, jc + 1)
                dve.tensor_tensor(we_lo[:, jc, :].rearrange("j (p q) -> j q p", q=DC),
                                  ps_o[1 - jc % 2][:, :].rearrange("j (q p) -> j q p", q=DC),
                                  we_hi[:, jc, :].bitcast(F32).rearrange("j (p q) -> j q p", q=DC),
                                  ALU.subtract).then_inc(we_lo_ready, 1)

            def combine(n, par, ops):
                up, low = val[:, par, :], lower[:, :]
                for op in ops:
                    if op == 0:
                        dve.wait_ge(lines, NLINES * n + 2)
                        wait(dve, t_done, n - 1)
                        ins = dve.tensor_tensor(up, ring[:, 0, :], ring[:, 1, :], ALU.max)
                    elif op == 1:
                        dve.wait_ge(lines, NLINES * n + 4)
                        wait(dve, combo, COMBOS * n)
                        ins = dve.scalar_tensor_tensor(out=low, in0=ring[:, 2, :], scalar=0.0, in1=ring[:, 3, :],
                                                       op0=ALU.min, op1=ALU.min)
                    elif op < COMBOS - 1:
                        dve.wait_ge(lines, NLINES * n + op + 3)
                        dve.wait_ge(combo, COMBOS * n + op - 1)
                        ins = (dve.tensor_tensor(up, up, ring[:, op - 2, :], ALU.max) if op % 2 == 0 else
                               dve.tensor_tensor(low, low, ring[:, op - 2, :], ALU.min))
                    else:
                        dve.wait_ge(combo, COMBOS * n + COMBOS - 1)
                        ins = dve.tensor_tensor(up, up, low, ALU.add)
                    ins.then_inc(combo, 1)

            def low_y(tile):
                dve.wait_ge(y_hi_ready, tile + 1)
                dve.tensor_tensor(y_lo[:, :, :].rearrange("p q t -> p (q t)"), ps_y[:, :],
                                  y_hi[:, :, :].bitcast(F32).rearrange("p q t -> p (q t)"), ALU.subtract
                                  ).then_inc(y_lo_ready, 1)

            def sum_x1(tile):
                dve.wait_ge(z_mm, tile + 1)
                dve.wait_ge(xb_ready, tile + 1)
                dve.tensor_tensor(x1s[:, :], ps_z[:, :], x1s[:, :], ALU.add).then_inc(x1_ready, 1)

            def mask_bx(tile):
                dve.wait_ge(bx_mm, tile + 1)
                wait(dve, bx_split, tile)
                dve.tensor_tensor(bx_f[:, :].rearrange("p (s c) -> p s c", c=CH),
                                  ps_u[:, 0:P].rearrange("p (s c) -> p s c", c=CH),
                                  mask[:, ds(PER * tile, PER)].unsqueeze(2).to_broadcast([P, PER, CH]), ALU.mult
                                  ).then_inc(bx_masked, 1)

            def iteration(i):
                a, b = 2 * i, 2 * i + 1
                for s in range(UPI):
                    if s in (0, UPI // 2):
                        low_y(a if s == 0 else b)
                    combine(UPI * i + s, s % 2, range(COMBOS))
                    if s in (1, 4):
                        sum_x1(a if s == 1 else b)
                    if s in (2, 5):
                        mask_bx(a if s == 2 else b)

            dve.wait_ge(mask_step, 3)
            iteration(0)
            with dve.Fori(1, ITER_A) as i:
                iteration(i)
            low_y(NT - 2)
            combine(TAIL_U, 0, range(COMBOS))
            sum_x1(NT - 2)
            combine(REST_U, 1, range(COMBOS))
            mask_bx(NT - 2)
            low_y(NT - 1)
            sum_x1(NT - 1)
            mask_bx(NT - 1)

            def product(g, b, k):
                q, rows, slot = chunk_no(g, b, k), REM if is_rest(g) else P, chunk_slot(g, b, k)
                dve.wait_ge(silu_ready, q + 1)
                dve.tensor_tensor(inter[0:rows, slot, :], ps_u[0:rows, :], silu_g[0:rows, slot, :], ALU.mult
                                  ).then_inc(inter_ready, 1)

            def product_low(g, b, k):
                q, rows, slot = chunk_no(g, b, k), REM if is_rest(g) else P, chunk_slot(g, b, k)
                dve.wait_ge(in_hi_ready, q + 1)
                dve.tensor_tensor(in_lo[0:rows, b % 2, k, :], inter[0:rows, slot, :],
                                  in_hi[0:rows, b % 2, k, :].bitcast(F32), ALU.subtract).then_inc(in_lo_ready, 1)

            def low_wd(n, gpar, k):
                dve.wait_ge(wd_hi_ready, n - REST_U + 1)
                dve.tensor_tensor(wd_lo[:, gpar, k, :], ps_t[:, :], wd_hi[:, gpar, k, :].bitcast(F32), ALU.subtract
                                  ).then_inc(wd_lo_ready, 1)

            def accumulate(g, t):
                r = t if is_rest(g) else NT * (g + 1) + t
                if is_rest(g) and t % TPB == 0:
                    dve.wait_ge(acc_in[t // TPB], 16)
                dve.wait_ge(down_mm, r + 1)
                dve.tensor_tensor(acc[:, t, :], ps_o[t % 2][:, :], acc[:, t, :], ALU.add).then_inc(added, 1)

            def group(g, gpar, last=False):
                n0, npar = next_units(g), 1 - gpar
                for b in range(NB):
                    for s, ops in enumerate(((0, 1, 2), (3, 4), (5,), (6,))):
                        work = next_chunk(g, b, s - 1, last)
                        if work:
                            product(*work)
                        if b < G and not last:
                            combine(n0 + b, (npar + b) % 2, ops)
                        if work:
                            product_low(*work)
                        if s == TPB - 1 and b > 0 and not last:
                            low_wd(n0 + b - 1, npar, b - 1)
                        accumulate(g, TPB * b + s)

            low_wd(REST_U, 1, 0)
            product(REST, 0, 0)
            product_low(REST, 0, 0)
            group(REST, 1)
            with dve.Fori(0, GROUPS // 2) as j:
                group(2 * j, 0)
                group(2 * j + 1, 1)
            group(GROUPS - 1, 0, last=True)

        @block.tensor
        def _(pe):
            pe.wait_ge(ident_ready, 2)
            pe.wait_ge(lb_scaled, 1)
            for q in range(DC):
                ins = pe.transpose(ps_t[:, q * P:(q + 1) * P], lbq[:, q, :, :].rearrange("p n r -> p (n r)"), ident[:, :])
            ins.then_inc(setup_t, 1)
            pe.wait_ge(ad_b_in, 16)
            for q in range(DC):
                ins = pe.transpose(ps_y[:, q * P:(q + 1) * P], ad_braw[:, q * P:(q + 1) * P], ident[:, :])
            ins.then_inc(setup_t, 1)
            pe.wait_ge(setup_evac, 1)
            for jc in range(DC):
                if jc == 1:
                    pe.wait_ge(setup_evac, 2)
                if jc >= 2:
                    pe.wait_ge(we_lo_ready, jc - 1)
                ps = ps_o[1 - jc % 2]
                for h in range(2):
                    pe.matmul(ps[:, h * HALF:(h + 1) * HALF], la[:, jc * P:(jc + 1) * P],
                              lbt[:, h * HALF:(h + 1) * HALF], start=True, stop=False)
                pe.wait_ge(w_in[jc % 2], 16 * (jc // 2 + 1))
                for q in range(DC):
                    ins = pe.matmul(ps[:, q * P:(q + 1) * P], w_chunk[jc % 2][:, q, :], ident[:, :],
                                    start=False, stop=q % 4 == 3)
                ins.then_inc(we_mm, 1)

            def cond_y(tile, slot, loads):
                pe.wait_ge(x_in[slot], 16 * loads)
                wait(pe, x1t_ready, tile)
                for jc in range(DC):
                    ins = pe.matmul(ps_y[:, jc * P:(jc + 1) * P], xs[:, slot, jc * P:(jc + 1) * P],
                                    cond_bd[:, ds(tile, 1), :].rearrange("p a n -> p (a n)"),
                                    start=True, stop=True)
                ins.then_inc(y_mm, 1)

            def ffn_z(tile):
                pe.wait_ge(y_lo_ready, tile + 1)
                wait(pe, x1_ready, tile)
                for jc in range(DC):
                    for p, (y, w) in enumerate(((y_hi, we_hi), (y_hi, we_lo), (y_lo, we_hi))):
                        for h in range(2):
                            ins = pe.matmul(ps_z[:, h * HALF:(h + 1) * HALF], y[:, jc, :],
                                            w[:, jc, h * HALF:(h + 1) * HALF],
                                            start=jc == 0 and p == 0, stop=jc == DC - 1 and p == 2)
                ins.then_inc(z_mm, 1)

            def turn_x1(tile):
                pe.wait_ge(x1_ready, tile + 1)
                for q in range(DC):
                    ins = pe.transpose(ps_y[:, q * P:(q + 1) * P], x1s[:, q * P:(q + 1) * P], ident[:, :])
                ins.then_inc(x1t_mm, 1)

            def adapter_bx(tile):
                pe.wait_ge(x1t_ready, tile + 1)
                wait(pe, bx_masked, tile)
                for q in range(DC):
                    ins = pe.matmul(ps_u[:, 0:P], ad_bt[:, q, :], x1t[:, q, :], start=q == 0, stop=q == DC - 1)
                ins.then_inc(bx_mm, 1)

            def turn_unit(n, par):
                pe.wait_ge(scaled, n + 1)
                wait(pe, wt_ready, n)
                v = val[:, par, :].rearrange("i (p q) -> i q p", q=DC)
                for q in range(DC):
                    ins = pe.transpose(ps_t[:, q * P:(q + 1) * P], v[:, q, :], ident[:, :])
                ins.then_inc(t_done, 1)

            def adapter_ga(n, par, chunk):
                pe.wait_ge(wt_ready, n + 1)
                if par == 0:
                    wait(pe, ga_evac, chunk)
                for q in range(DC):
                    ins = pe.matmul(ps_g[:, par * P:(par + 1) * P], ad_at[:, q, :, :].rearrange("p n r -> p (n r)"), wt[:, par, q, :],
                                    start=q == 0, stop=q == DC - 1)
                ins.then_inc(ga_mm, 1)

            def iteration(i):
                a, b, n, c = 2 * i, 2 * i + 1, UPI * i, G * i
                ffn_z(a)
                turn_unit(n, 0)
                adapter_ga(n, 0, c)
                turn_unit(n + 1, 1)
                turn_x1(a)
                adapter_ga(n + 1, 1, c)
                adapter_bx(a)
                cond_y(b, 1, i + 1)
                turn_unit(n + 2, 0)
                ffn_z(b)
                adapter_ga(n + 2, 0, c + 1)
                turn_unit(n + 3, 1)
                adapter_ga(n + 3, 1, c + 1)
                turn_unit(n + 4, 0)
                turn_x1(b)
                adapter_ga(n + 4, 0, c + 2)
                adapter_bx(b)
                cond_y(a + 2, 0, i + 2)
                turn_unit(n + 5, 1)
                adapter_ga(n + 5, 1, c + 2)

            pe.wait_ge(bd_in, 16 * SAMPLES)
            pe.wait_ge(we_lo_ready, DC)
            cond_y(0, 0, 1)
            pe.wait_ge(ad_at_ready, 1)
            iteration(0)
            with pe.Fori(1, ITER_A) as i:
                iteration(i)
            ffn_z(NT - 2)
            turn_unit(TAIL_U, 0)
            turn_x1(NT - 2)
            adapter_ga(TAIL_U, 0, CHUNKS)
            adapter_bx(NT - 2)
            cond_y(NT - 1, 1, NT // 2)
            ffn_z(NT - 1)
            turn_x1(NT - 1)
            adapter_bx(NT - 1)

            def turn_down(n, par):
                pe.wait_ge(scaled, n + 1)
                wait(pe, wd_lo_ready, n - REST_U)
                for t in range(DC):
                    ins = pe.transpose(ps_t[:, t * P:(t + 1) * P], val[:, par, t * P:(t + 1) * P], ident[:, :])
                ins.then_inc(t_done, 1)

            def gate_up(g, b, k):
                q = chunk_no(g, b, k)
                if b == 0:
                    loads = 1 if is_rest(g) else g + 1 + (k == 0)
                    pe.wait_ge(stage_in[k], 32 * loads)
                wait(pe, silu_ready, q)
                wait(pe, inter_ready, q)
                cols = slice(b * HALF, (b + 1) * HALF)
                for m, ps in enumerate((ps_g, ps_u)):
                    for p, (w, v) in enumerate(((st_hi, bx_hi), (st_hi, bx_lo), (st_lo, bx_hi))):
                        ins = pe.matmul(ps[:, :], w[:, k, m, :], v[:, cols], start=p == 0, stop=p == 2)
                ins.then_inc(gu_mm, 1)

            def down(g, b, s, gpar):
                chunks, rows = (1, REM) if is_rest(g) else (G, P)
                t = TPB * b + s
                if s == 0:
                    pe.wait_ge(in_lo_ready, chunk_no(g, b, chunks - 1) + 1)
                if s == 0 and b == 0:
                    pe.wait_ge(wd_lo_ready, 1 if is_rest(g) else 1 + G * (g + 1))
                wait(pe, added, (t if is_rest(g) else NT * (g + 1) + t) - 1)
                for k in range(chunks):
                    for p, (v, w) in enumerate(((in_hi, wd_hi), (in_hi, wd_lo), (in_lo, wd_hi))):
                        for h in range(2):
                            ins = pe.matmul(ps_o[t % 2][:, h * HALF:(h + 1) * HALF],
                                            v[0:rows, b % 2, k, s * P:(s + 1) * P],
                                            w[0:rows, gpar, k, h * HALF:(h + 1) * HALF],
                                            start=k == 0 and p == 0, stop=k == chunks - 1 and p == 2)
                ins.then_inc(down_mm, 1)

            def group(g, gpar, last=False):
                n0, npar = next_units(g), 1 - gpar
                for b in range(NB):
                    for s in range(TPB):
                        down(g, b, s, gpar)
                        work = next_chunk(g, b, s, last)
                        if work:
                            gate_up(*work)
                        if s == 1 and b > 0 and not last:
                            turn_down(n0 + b - 1, (npar + b - 1) % 2)

            pe.wait_ge(wt_ready, REST_U)
            turn_down(REST_U, 1)
            pe.wait_ge(ga_evac, CHUNKS + 1)
            pe.wait_ge(bx_split, NT)
            gate_up(REST, 0, 0)
            group(REST, 1)
            with pe.Fori(0, GROUPS // 2) as j:
                group(2 * j, 0)
                group(2 * j + 1, 1)
            group(GROUPS - 1, 0, last=True)


_INS = ["x", "itok_B_0_15", "itok_B_3_7", "L0_cond_weights", "L0_ffn_lora_A", "L0_ffn_lora_B", "L0_ffn_W",
        "L0_ffn_bias", "L0_ffn_lora_weights", "L1_cond_A", "L1_cond_B", "L1_ffn_gate_codes",
        "L1_ffn_gate_scales", "L1_ffn_up_codes", "L1_ffn_up_scales", "L1_ffn_down_codes", "L1_ffn_down_scales"]


def kernel(**inputs):
    import numpy as _np
    import concourse.bacc as _bacc
    from concourse import mybir as _mybir
    from concourse.bass_utils import run_bass_kernel_spmd as _run

    nc = _bacc.Bacc("TRN2", target_bir_lowering=False, num_devices=1)
    arrays, args = {}, []
    for name in _INS:
        a = _np.ascontiguousarray(inputs[name])
        arrays[f"in_{name}"] = a
        args.append(nc.dram_tensor(f"in_{name}", a.shape, _mybir.dt.from_np(a.dtype), kind="ExternalInput").ap())
    shape = inputs["x"].shape
    out = nc.dram_tensor("out", shape, _mybir.dt.float32, kind="ExternalOutput").ap()
    adaln_ffn(nc, *args, out)
    r = _run(nc, [arrays], core_ids=[0])
    return r.results[0]["out"]
```

```python
from contextlib import ExitStack

import numpy as np

import concourse.bass as bass
from concourse import mybir

F32 = mybir.dt.float32
F32R = mybir.dt.float32r
I32 = mybir.dt.int32
ALU = mybir.AluOpType
ACT = mybir.ActivationFunctionType
ds = bass.ds

NF4 = [-1.0, -0.6961928009986877, -0.5250730514526367, -0.39491748809814453, -0.28444138169288635,
       -0.18477343022833234, -0.09105003625154495, 0.0, 0.07958029955625534, 0.16093020141124725,
       0.24611230194568634, 0.33791524171829224, 0.44070982933044434, 0.5626170039176941,
       0.7229568362236023, 1.0]
MID = 8
UPPER = [(0.08134990185499191, 0.07958029955625534), (0.0918029248714447, 0.06250645220279694),
         (0.12190713733434677, -0.046918708831071854), (0.2770431339740753, -0.9393019676208496)]
LOWER = [(0.09105003625154495, 0.09105003625154495), (0.09966794401407242, 0.11423040181398392),
         (0.1301555186510086, 0.2558600902557373), (0.30380719900131226, 1.430457592010498)]
LINES = [UPPER[1], LOWER[0], LOWER[1], UPPER[2], LOWER[2], UPPER[3], LOWER[3]]
NLINES = len(LINES)
TAKEN_BY = [1, 2, 2, 3, 4, 5, 6]
COMBOS = 7


def check_lines():
    for code, level in enumerate(NF4):
        at = [np.float32(np.float64(code - MID) * m + c) for m, c in UPPER + LOWER]
        at[0] = np.float32(np.float32(code - MID) * np.float32(UPPER[0][0])) + np.float32(UPPER[0][1])
        up, low = max(0.0, *at[:4]), min(0.0, *at[4:])
        assert np.float32(up + low) == np.float32(level)


def adaln_ffn(nc, x, cond_id, adapter_id, cond_w, lora_a, lora_b, w0, bias0, lora_w, ad_a, ad_b,
              gate_codes, gate_scales, up_codes, up_scales, down_codes, down_scales, out):
    check_lines()
    SAMPLES, CH, D = x.shape
    P = 128
    ROWS = SAMPLES * CH
    NT = ROWS // P
    PER = P // CH
    DC = D // P
    HALF = 512
    NCOND = cond_w.shape[0]
    NAD, RANK, _ = ad_b.shape
    NR = NAD * RANK
    LORA_SCALE = 32 / lora_a.shape[1]
    HID = gate_codes.shape[0]
    BLK = D // gate_scales.shape[1]
    SB = gate_scales.shape[1]
    DSB = down_scales.shape[1]
    CHUNKS = HID // P
    REM = HID - CHUNKS * P
    G = 3
    GROUPS = CHUNKS // G
    NB = ROWS // HALF
    TPB = HALF // P
    ITER_A = 7
    UPI = 2 * CHUNKS // ITER_A
    TAIL_U = 2 * CHUNKS
    REST_U = TAIL_U + 1
    DOWN_U = REST_U + 1
    UNITS = DOWN_U + CHUNKS
    assert NR == P and 2 * REM == P and GROUPS * G == CHUNKS and ITER_A * UPI == TAIL_U
    assert UPI == 6 and NT == 2 * ITER_A + 2 and GROUPS % 2 == 1 and BLK == 64 and RANK == 16
    RING = 4

    x_rows = x.rearrange("s c d -> (s c) d")
    out_rows = out.rearrange("s c d -> (s c) d")
    x1_dram = nc.dram_tensor("x1_scratch", [ROWS, D], F32, kind="Internal").ap()
    ga_hi_dram = nc.dram_tensor("ga_hi_scratch", [CHUNKS + 1, P, 2 * P], F32, kind="Internal").ap()
    ga_lo_dram = nc.dram_tensor("ga_lo_scratch", [CHUNKS + 1, P, 2 * P], F32, kind="Internal").ap()

    with ExitStack() as ctx:
        def sb(name, shape, dt, where=ctx):
            return where.enter_context(nc.sbuf_tensor(name, shape, dt))

        def sem(name):
            return ctx.enter_context(nc.semaphore(name))

        ident = sb("ident", [P, P], F32)
        mid = sb("mid", [P, 1], I32)
        one = sb("one", [P, 1], F32)
        line_c = sb("line_c", [P, NLINES], F32)
        gu_scales = sb("gu_scales", [P, CHUNKS + 1, 2, SB], F32)
        d_scales = sb("d_scales", [P, DC, DSB], F32)
        mask = sb("mask", [P, SAMPLES], F32)
        bx_hi = sb("bx_hi", [P, ROWS], F32R)
        bx_lo = sb("bx_lo", [P, ROWS], F32R)
        codes = sb("codes", [P, 2, D], I32)
        ring = sb("ring", [P, RING, D], F32)
        lower = sb("lower", [P, 2, D], F32)
        val = sb("val", [P, 2, D], F32)

        phase_a = ExitStack()
        we_hi = sb("we_hi", [P, DC, D], F32R, phase_a)
        we_lo = sb("we_lo", [P, DC, D], F32R, phase_a)
        xs = sb("xs", [P, 2, D], F32, phase_a)
        x1s = sb("x1s", [P, D], F32, phase_a)
        x1t = sb("x1t", [P, DC, P], F32, phase_a)
        y_hi = sb("y_hi", [P, DC, P], F32R, phase_a)
        y_lo = sb("y_lo", [P, DC, P], F32R, phase_a)
        cond_bd = sb("cond_bd", [P, NT, P], F32, phase_a)
        ad_bt = sb("ad_bt", [P, DC, P], F32, phase_a)
        ad_at = sb("ad_at", [P, DC, NAD, RANK], F32, phase_a)
        ring_more = sb("ring_more", [P, NLINES - RING, D], F32, phase_a)
        codes_more = sb("codes_more", [P, D], I32, phase_a)
        val_more = sb("val_more", [P, D], F32, phase_a)
        wt = sb("wt", [P, 2, DC, P], F32, phase_a)
        bias_b = sb("bias_b", [P, D], F32, phase_a)
        ga_hi = sb("ga_hi", [P, 2 * P], F32R, phase_a)
        ga_lo = sb("ga_lo", [P, 2 * P], F32R, phase_a)
        la = sb("la", [P, D], F32, phase_a)
        lb = sb("lb", [P, NAD, DC, RANK], F32, phase_a)
        lw = sb("lw", [P, NAD], F32, phase_a)
        cond_ids = sb("cond_ids", [1, SAMPLES], I32, phase_a)
        ad_ids = sb("ad_ids", [P, SAMPLES], I32, phase_a)
        part_i = sb("part_i", [P, 1], I32, phase_a)
        part_ad = sb("part_ad", [P, 1], I32, phase_a)
        part_f = sb("part_f", [P, 1], F32, phase_a)
        lbt = ring_more[:, 0, :]
        ad_braw = val[:, 1, :]
        ad_araw = ring[:, 1, :].rearrange("p (n q r) -> p n q r", n=NAD, q=DC)
        lbq = ring[:, 0, :].rearrange("p (q n r) -> p q n r", n=NAD, q=DC)
        ga_f = la[:, 0:2 * P]
        bx_f = la[:, 2 * P:3 * P]
        w_chunk = [x1s[:, :].rearrange("p (q j) -> p q j", q=DC), x1t[:, :, :]]
        phase_a.close()

        acc = sb("acc", [P, NT, D], F32)
        wd_hi = sb("wd_hi", [P, 2, G, D], F32R)
        wd_lo = sb("wd_lo", [P, 2, G, D], F32R)
        in_hi = sb("in_hi", [P, 2, G, HALF], F32R)
        in_lo = sb("in_lo", [P, 2, G, HALF], F32R)
        st_hi = sb("st_hi", [P, G, 2, P], F32R)
        st_lo = sb("st_lo", [P, G, 2, P], F32R)
        inter = sb("inter", [P, 2, HALF], F32)

        ps_y = ctx.enter_context(nc.psum_tensor("ps_y", [P, D], F32))
        ps_z = ctx.enter_context(nc.psum_tensor("ps_z", [P, D], F32))
        ps_t = ctx.enter_context(nc.psum_tensor("ps_t", [P, D], F32))
        ps_g = ctx.enter_context(nc.psum_tensor("ps_g", [P, HALF], F32))
        ps_u = ctx.enter_context(nc.psum_tensor("ps_u", [P, HALF], F32))
        ps_o = [ps_y, ps_z]

        ids_in = sem("ids_in")
        ad_ids_in = sem("ad_ids_in")
        lora_in = sem("lora_in")
        ad_b_in = sem("ad_b_in")
        ad_a_in = sem("ad_a_in")
        bias_in = sem("bias_in")
        scales_in = sem("scales_in")
        bd_in = sem("bd_in")
        w_in = [sem(f"w_in{k}") for k in range(2)]
        x_in = [sem(f"x_in{k}") for k in range(2)]
        codes_in = [sem(f"codes_in{k}") for k in range(3)]
        down_codes_in = [sem(f"down_codes_in{k}") for k in range(2)]
        stage_in = [sem(f"stage_in{k}") for k in range(G)]
        acc_in = [sem(f"acc_in{k}") for k in range(NB)]
        x1_out = sem("x1_out")
        ga_out = sem("ga_out")
        out_done = sem("out_done")
        consts_ready = sem("consts_ready")
        ident_ready = sem("ident_ready")
        bd_zeroed = sem("bd_zeroed")
        line_c_ready = sem("line_c_ready")
        part_ready = sem("part_ready")
        mask_step = sem("mask_step")
        lw_ready = sem("lw_ready")
        ad_at_ready = sem("ad_at_ready")
        lb_scaled = sem("lb_scaled")
        setup_t = sem("setup_t")
        setup_evac = sem("setup_evac")
        we_mm = sem("we_mm")
        we_hi_ready = sem("we_hi_ready")
        we_lo_ready = sem("we_lo_ready")
        shifted = sem("shifted")
        lines = sem("lines")
        combo = sem("combo")
        summed = sem("summed")
        scaled = sem("scaled")
        t_done = sem("t_done")
        wt_ready = sem("wt_ready")
        ga_mm = sem("ga_mm")
        ga_evac = sem("ga_evac")
        ga_step = sem("ga_step")
        ga_split = sem("ga_split")
        y_mm = sem("y_mm")
        y_hi_ready = sem("y_hi_ready")
        y_lo_ready = sem("y_lo_ready")
        z_mm = sem("z_mm")
        xb_ready = sem("xb_ready")
        x1_ready = sem("x1_ready")
        x1t_mm = sem("x1t_mm")
        x1t_ready = sem("x1t_ready")
        bx_mm = sem("bx_mm")
        bx_masked = sem("bx_masked")
        bx_step = sem("bx_step")
        bx_split = sem("bx_split")
        wd_hi_ready = sem("wd_hi_ready")
        wd_lo_ready = sem("wd_lo_ready")
        gu_mm = sem("gu_mm")
        silu_ready = sem("silu_ready")
        inter_ready = sem("inter_ready")
        in_hi_ready = sem("in_hi_ready")
        in_lo_ready = sem("in_lo_ready")
        down_mm = sem("down_mm")
        added = sem("added")

        REST = -1

        def chunk_no(g, b, k):
            return b if is_rest(g) else NB * (1 + G * g) + G * b + k

        def is_rest(g):
            return isinstance(g, int) and g == REST

        def next_chunk(g, b, k, last):
            if k < 0 or k >= G or (b == NB - 1 and last):
                return None
            if b == NB - 1:
                return (0 if is_rest(g) else g + 1), 0, k
            return (g, b + 1, k) if k == 0 or not is_rest(g) else None

        def chunk_slot(g, b, k):
            return b % 2 if is_rest(g) else (G * b + k) % 2

        def next_units(g):
            return DOWN_U if is_rest(g) else DOWN_U + G * (g + 1)

        def val_slot(n3):
            return val_more[:, :] if n3 == 2 else val[:, n3, :]

        def codes_slot(n3):
            return codes_more[:, :] if n3 == 2 else codes[:, n3, :]

        def line_slot(k, own):
            return ring_more[:, k - RING, :] if own and k >= RING else ring[:, k % RING, :]

        def wait(eng, semaphore, count):
            if not isinstance(count, int) or count > 0:
                eng.wait_ge(semaphore, count)

        block = ctx.enter_context(nc.Block())

        @block.sync
        def _(sp):
            def load_x(tile, slot):
                if not isinstance(tile, int) or tile > 1:
                    sp.wait_ge(y_mm, tile - 1)
                    sp.wait_ge(xb_ready, tile - 1)
                sp.dma_start(xs[:, slot, :], x_rows[ds(tile * P, P), :]).then_inc(x_in[slot], 16)

            def load_gu(n, slot, up, chunk):
                if not isinstance(n, int) or n > 2:
                    sp.wait_ge(lines, NLINES * (n - 2) + 1)
                sp.dma_start(codes_slot(slot), (up_codes if up else gate_codes)[ds(chunk * P, P), :]
                             ).then_inc(codes_in[slot], 16)

            def load_down(n, slot, col, width, count, signal):
                sp.wait_ge(lines, count)
                sp.dma_start(codes[:, slot, :].rearrange("p (t i) -> p t i", t=DC)[:, :, 0:width],
                             down_codes.rearrange("(t p) i -> p t i", p=P)[:, :, ds(col, width)]
                             ).then_inc(signal, 16)

            def load_down_chunk(c, par, behind_a=0):
                n = DOWN_U + c
                load_down(n, par, c * P, P, NLINES * (n - 1) + behind_a, down_codes_in[par])

            def store_x1(tile):
                sp.wait_ge(x1_ready, tile + 1)
                sp.dma_start(x1_dram[ds(tile * P, P), :], x1s[:, :]).then_inc(x1_out, 16)

            def store_ga(chunk):
                sp.wait_ge(ga_split, chunk + 1)
                for src, dst in ((ga_hi, ga_hi_dram), (ga_lo, ga_lo_dram)):
                    sp.dma_start(dst[ds(chunk, 1), :, :].rearrange("a p n -> p a n"),
                                 src[:, :].bitcast(F32).rearrange("p (a n) -> p a n", a=1)
                                 ).then_inc(ga_out, 16)

            load_gu(0, 0, 0, 0)
            sp.dma_start(cond_ids[:, :], cond_id.rearrange("(a s) -> a s", a=1)).then_inc(ids_in, 16)
            load_x(0, 0)
            load_x(1, 1)
            load_gu(1, 1, 1, 0)
            load_gu(2, 2, 0, 1)
            sp.wait_ge(ids_in, 16)
            sp.wait_ge(bd_zeroed, 1)
            with sp.Fori(0, NT) as m:
                for half in range(PER):
                    cid = sp.value_load(cond_ids[0:1, ds(PER * m + half, 1)], min_val=0, max_val=NCOND - 1)
                    sp.dma_start(cond_bd[half * CH:(half + 1) * CH, ds(m, 1), half * CH:(half + 1) * CH],
                                 cond_w[ds(cid, 1), :, :].rearrange("a c e -> c a e")).then_inc(bd_in, 16)

            def iteration(i, first=False, last=False):
                for s in range(UPI):
                    n = UPI * i + s + 3
                    if not last or s < UPI // 2:
                        load_gu(n, s % 3, (s + 1) % 2, G * i + (s + 3) // 2)
                    elif s == UPI // 2:
                        sp.wait_ge(lines, NLINES * (n - 2) + 1)
                        for half, src in enumerate((gate_codes, up_codes)):
                            sp.dma_start(codes[half * REM:(half + 1) * REM, 0, :], src[CHUNKS * P:HID, :]
                                         ).then_inc(codes_in[0], 16)
                    elif s == UPI // 2 + 1:
                        load_down(n, 1, CHUNKS * P, REM, NLINES * (n - 2) + 1, codes_in[1])
                    if s == 1 and not first:
                        store_ga(G * i - 1)
                    if s % 3 == 2:
                        load_x(2 * i + 2 + s // 3, s // 3)
                        store_x1(2 * i + s // 3)
                    if s == 3:
                        store_ga(G * i)
                    if s == 5:
                        store_ga(G * i + 1)

            iteration(0, first=True)
            with sp.Fori(1, ITER_A - 1) as i:
                iteration(i)
            iteration(ITER_A - 1, last=True)

            load_down_chunk(0, 0, 1)
            store_ga(CHUNKS - 1)
            store_x1(NT - 2)
            store_ga(CHUNKS)
            store_x1(NT - 1)
            sp.wait_ge(z_mm, NT)
            sp.wait_ge(x1_out, 16 * NT)
            for b in range(NB):
                sp.dma_start(acc[:, b * TPB:(b + 1) * TPB, :],
                             x1_dram[b * HALF:(b + 1) * HALF, :].rearrange("(t p) d -> p t d", p=P)
                             ).then_inc(acc_in[b], 16)
            load_down_chunk(1, 1, 1)
            with sp.Fori(1, CHUNKS // 2) as j:
                for par in range(2):
                    load_down_chunk(2 * j + par, par)
            load_down_chunk(CHUNKS - 1, 0)
            for t in range(NT):
                sp.wait_ge(added, NT * GROUPS + t + 1)
                sp.dma_start(out_rows[t * P:(t + 1) * P, :], acc[:, t, :]).then_inc(out_done, 16)
            sp.wait_ge(out_done, 16 * NT)

        @block.gpsimd
        def _(pool):
            pool.memset(ident[:, :], 0.0).then_inc(ident_ready, 1)
            pool.wait_ge(ident_ready, 1)
            pool.affine_select(out=ident[:, :], in_=ident[:, :], compare_op=ALU.not_equal, fill=1.0, base=0,
                               pattern=[[-1, P]], channel_multiplier=1).then_inc(ident_ready, 1)
            pool.iota(part_i[:, :], pattern=[[0, 1]], base=0, channel_multiplier=1).then_inc(part_ready, 1)

            def shift(slot, signal, loads):
                pool.wait_ge(signal, 16 * loads)
                pool.tensor_tensor(codes_slot(slot), codes_slot(slot), mid[:, :].to_broadcast([P, D]), ALU.subtract
                                   ).then_inc(shifted, 1)

            def shift_down(par, pair):
                shift(par, down_codes_in[par], pair + 1)

            def scale(n, par, slot, scales, blocks=None):
                v = val_slot(slot)
                pool.wait_ge(combo, COMBOS * (n + 1))
                pool.tensor_tensor(v, v, lower[:, par, :], ALU.add).then_inc(summed, 1)
                pool.wait_ge(summed, n + 1)
                b = v.rearrange("p (b j) -> p b j", j=BLK) if blocks is None else blocks(v)
                pool.tensor_tensor(b, b, scales, ALU.mult).then_inc(scaled, 1)

            def gu_scale(chunk, kind):
                return gu_scales[:, ds(chunk, 1), kind, :].rearrange("p a b -> p (a b)").unsqueeze(2
                                 ).to_broadcast([P, SB, BLK])

            def add_bias(tile, slot, i):
                pool.wait_ge(x_in[slot], 16 * (i + 1))
                wait(pool, x1_out, 16 * tile)
                wait(pool, x1t_mm, tile)
                pool.tensor_tensor(x1s[:, :], xs[:, slot, :], bias_b[:, :], ALU.add).then_inc(xb_ready, 1)

            def split_ga(chunk):
                pool.wait_ge(ga_evac, chunk + 1)
                wait(pool, ga_out, 32 * chunk)
                pool.tensor_tensor(ga_hi[:, :], ga_f, one[:, :].to_broadcast([P, 2 * P]), ALU.mult
                                   ).then_inc(ga_step, 1)
                pool.wait_ge(ga_step, chunk + 1)
                pool.tensor_tensor(ga_lo[:, :], ga_f, ga_hi[:, :].bitcast(F32), ALU.subtract
                                   ).then_inc(ga_split, 1)

            def split_bx(tile):
                hi, lo = bx_hi[:, ds(tile * P, P)], bx_lo[:, ds(tile * P, P)]
                pool.wait_ge(bx_masked, tile + 1)
                pool.tensor_tensor(hi, bx_f, one[:, :].to_broadcast([P, P]), ALU.mult
                                   ).then_inc(bx_step, 1)
                pool.wait_ge(bx_step, tile + 1)
                pool.tensor_tensor(lo, bx_f, hi.bitcast(F32), ALU.subtract).then_inc(bx_split, 1)

            def iteration(i, first=False, last=False):
                for s in range(UPI):
                    n, par = UPI * i + s, s % 2
                    if s % 3 == 1:
                        add_bias(2 * i + s // 3, s // 3, i)
                    slot = (s + 2) % 3
                    shift(slot, codes_in[slot], 2 * i + (s + 2) // 3 + 1 + (last and s == UPI - 2))
                    if s == 5 or (s == 2 and not first):
                        split_bx(2 * i + s // 3 - 1)
                    if s % 2 == 1 and (s > 1 or not first):
                        split_ga(G * i + s // 2 - 1)
                    scale(n, par, s % 3, gu_scale(G * i + s // 2, par))

            pool.memset(mid[:, :], MID).then_inc(consts_ready, 1)
            pool.memset(one[:, :], 1.0).then_inc(consts_ready, 1)
            pool.wait_ge(consts_ready, 2)
            shift(0, codes_in[0], 1)
            shift(1, codes_in[1], 1)
            pool.wait_ge(bias_in, 16)
            pool.wait_ge(scales_in, 16 * 5)
            pool.wait_ge(we_mm, DC)
            iteration(0, first=True)
            with pool.Fori(1, ITER_A - 1) as i:
                iteration(i)
            iteration(ITER_A - 1, last=True)

            def scale_down(c, n, par):
                scale(n, par, par, d_scales[:, :, ds(2 * c, 2)].unsqueeze(3).to_broadcast([P, DC, 2, BLK]),
                      lambda v: v.rearrange("p (t b j) -> p t b j", t=DC, j=BLK))

            shift_down(0, 0)
            add_bias(NT - 2, 0, ITER_A)
            scale(TAIL_U, 0, 0, gu_scale(CHUNKS, 0))
            split_bx(NT - 3)
            split_ga(CHUNKS - 1)
            scale(REST_U, 1, 1, d_scales[:, :, DSB - 1:DSB].to_broadcast([P, DC, BLK]),
                  lambda v: v.rearrange("p (t j) -> p t j", t=DC)[:, :, 0:REM])
            split_ga(CHUNKS)
            add_bias(NT - 1, 1, ITER_A)
            split_bx(NT - 2)
            split_bx(NT - 1)
            shift_down(1, 0)
            with pool.Fori(0, (CHUNKS - 3) // 2) as j:
                for par in range(2):
                    c = 2 * j + par
                    shift_down(par, j + 1)
                    scale_down(c, DOWN_U + c, par)
            for c in range(CHUNKS - 3, CHUNKS):
                if c + 2 < CHUNKS:
                    shift_down(c % 2, c // 2 + 1)
                scale_down(c, DOWN_U + c, c % 2)

        @block.scalar
        def _(act):
            act.dma_start(lb[:, :, :, :].rearrange("p n q r -> p n (q r)"),
                          lora_b.rearrange("n (p q) r -> p n (q r)", p=P)).then_inc(lora_in, 16)
            act.dma_start(lw[:, :], lora_w.partition_broadcast(P)).then_inc(lora_in, 16)
            act.dma_start(la[:, :], lora_a.rearrange("n r d -> (n r) d")).then_inc(lora_in, 16)
            w_qj = w0.rearrange("(p q) j -> p q j", p=P)

            def load_w(jc):
                if jc >= 2:
                    act.wait_ge(we_mm, jc - 1)
                act.dma_start(w_chunk[jc % 2], w_qj[:, :, jc * P:(jc + 1) * P]).then_inc(w_in[jc % 2], 16)

            load_w(0)
            load_w(1)
            act.dma_start(ad_araw.rearrange("p n q r -> p n (q r)"),
                          ad_a.rearrange("n (p q) r -> p n (q r)", p=P)).then_inc(ad_a_in, 16)
            act.dma_start(ad_braw, ad_b.rearrange("n r d -> (n r) d")).then_inc(ad_b_in, 16)
            act.dma_start(ad_ids[:, :], adapter_id.partition_broadcast(P)).then_inc(ad_ids_in, 16)
            act.dma_start(bias_b[:, :], bias0.partition_broadcast(P)).then_inc(bias_in, 16)
            for kind, src in enumerate((gate_scales, up_scales)):
                act.dma_start(gu_scales[:, 0:CHUNKS, kind, :],
                              src[0:CHUNKS * P, :].rearrange("(c p) b -> p c b", p=P)).then_inc(scales_in, 16)
                act.dma_start(gu_scales[kind * REM:(kind + 1) * REM, CHUNKS, 0, :], src[CHUNKS * P:HID, :]
                              ).then_inc(scales_in, 16)
            act.dma_start(d_scales[:, :, :], down_scales.rearrange("(t p) b -> p t b", p=P)
                          ).then_inc(scales_in, 16)

            def line(n, k, slot, own=True):
                if k == 0:
                    act.wait_ge(shifted, n + 1)
                if own:
                    wait(act, combo, COMBOS * (n - 1) + TAKEN_BY[k] + 1)
                elif k >= RING:
                    act.wait_ge(combo, COMBOS * n + TAKEN_BY[k - RING] + 1)
                else:
                    before = max(j for j in range(NLINES) if j % RING == k)
                    act.wait_ge(combo, COMBOS * (n - 1) + TAKEN_BY[before] + 1)
                slope, _ = LINES[k]
                act.activation(line_slot(k, own), codes_slot(slot), ACT.Identity,
                               bias=line_c[:, k:k + 1], scale=slope).then_inc(lines, 1)

            def some_lines(n, slot, ks, own=True):
                for k in ks:
                    line(n, k, slot, own)

            def evac_t(n, par):
                act.wait_ge(t_done, n + 1)
                wait(act, ga_mm, n - 1)
                act.activation(wt[:, par, :, :], ps_t[:, :].rearrange("p (q i) -> p q i", q=DC), ACT.Copy
                               ).then_inc(wt_ready, 1)

            def evac_y(tile):
                act.wait_ge(y_mm, tile + 1)
                wait(act, z_mm, tile)
                act.activation(y_hi[:, :, :].rearrange("p q t -> p (q t)"), ps_y[:, :], ACT.Copy
                               ).then_inc(y_hi_ready, 1)

            def evac_x1t(tile):
                act.wait_ge(x1t_mm, tile + 1)
                wait(act, bx_mm, tile)
                act.activation(x1t[:, :, :].rearrange("p q t -> p (q t)"), ps_z[:, :], ACT.Copy
                               ).then_inc(x1t_ready, 1)

            def evac_ga(chunk):
                act.wait_ge(ga_mm, 2 * chunk + 2)
                wait(act, ga_split, chunk)
                act.activation(ga_f, ps_g[:, 0:2 * P], ACT.Copy).then_inc(ga_evac, 1)

            act.wait_ge(setup_t, 1)
            act.activation(lbt, ps_t[:, :], ACT.Copy).then_inc(setup_evac, 1)
            act.wait_ge(setup_t, 2)
            act.activation(ad_bt[:, :, :].rearrange("p q t -> p (q t)"), ps_y[:, :], ACT.Copy
                           ).then_inc(setup_evac, 1)
            act.wait_ge(line_c_ready, NLINES)
            act.wait_ge(ad_at_ready, 1)
            for jc in range(DC):
                if jc < RING:
                    line(0, jc, 0)
                if jc + 2 < DC:
                    load_w(jc + 2)
                act.wait_ge(we_mm, jc + 1)
                act.activation(we_hi[:, jc, :].rearrange("j (p q) -> j q p", q=DC),
                               ps_o[1 - jc % 2][:, :].rearrange("j (q p) -> j q p", q=DC), ACT.Copy
                               ).then_inc(we_hi_ready, 1)
            evac_y(0)
            some_lines(0, 0, range(RING, NLINES))

            def iteration(i, first=False):
                for s in range(UPI):
                    n, par, tile = UPI * i + s, s % 2, 2 * i + s // 3
                    some_lines(n + 1, (s + 1) % 3, range(2))
                    if s == 3 or (s == 0 and not first):
                        evac_x1t(tile - 1)
                    some_lines(n + 1, (s + 1) % 3, range(2, 5))
                    if s % 2 == 1 and (s > 1 or not first):
                        evac_ga(G * i + s // 2 - 1)
                    if s % 3 == 2:
                        evac_y(tile + 1)
                    some_lines(n + 1, (s + 1) % 3, range(5, NLINES))
                    if s > 0 or not first:
                        evac_t(n - 1, 1 - par)

            iteration(0, first=True)
            with act.Fori(1, ITER_A) as i:
                iteration(i)

            some_lines(REST_U, 1, range(2))
            evac_x1t(NT - 3)
            some_lines(REST_U, 1, range(2, NLINES))
            evac_t(TAIL_U - 1, 1)
            evac_ga(CHUNKS - 1)
            evac_y(NT - 1)
            evac_t(TAIL_U, 0)
            evac_x1t(NT - 2)
            act.wait_ge(ga_mm, TAIL_U + 1)
            act.wait_ge(ga_split, CHUNKS)
            act.activation(ga_f[:, 0:P], ps_g[:, 0:P], ACT.Copy)
            act.activation(ga_f[:, P:P + REM], ps_g[:, REM:P], ACT.Copy)
            act.activation(ga_f[:, P + REM:2 * P], ps_g[:, 0:REM], ACT.Copy).then_inc(ga_evac, 1)
            evac_x1t(NT - 1)

            def stage(g, k):
                chunk = CHUNKS if is_rest(g) else G * g + k
                for dst, src in ((st_hi, ga_hi_dram), (st_lo, ga_lo_dram)):
                    act.dma_start(dst[:, k:k + 1, :, :].bitcast(F32).rearrange("p a m i -> p a (m i)"),
                                  src[ds(chunk, 1), :, :].rearrange("a p n -> p a n")).then_inc(stage_in[k], 16)

            def silu(g, b, k):
                q, rows = chunk_no(g, b, k), REM if is_rest(g) else P
                act.wait_ge(gu_mm, q + 1)
                wait(act, in_lo_ready, q - 1)
                act.activation(inter[0:rows, chunk_slot(g, b, k), :], ps_g[0:rows, :], ACT.Silu
                               ).then_inc(silu_ready, 1)

            def inter_hi(g, b, k):
                q, rows = chunk_no(g, b, k), REM if is_rest(g) else P
                act.wait_ge(inter_ready, q + 1)
                act.activation(in_hi[0:rows, b % 2, k, :], inter[0:rows, chunk_slot(g, b, k), :], ACT.Copy
                               ).then_inc(in_hi_ready, 1)

            def evac_wd(n, gpar, k):
                act.wait_ge(t_done, n + 1)
                act.activation(wd_hi[:, gpar, k, :], ps_t[:, :], ACT.Copy).then_inc(wd_hi_ready, 1)

            def group(g, gpar, last=False):
                n0, npar = next_units(g), 1 - gpar
                for b in range(NB):
                    for s in range(TPB):
                        if b == 0 and s == 0 and not last:
                            some_lines(n0, npar, range(RING), own=False)
                        work = next_chunk(g, b, s - 1, last)
                        if work:
                            silu(*work)
                            if b == NB - 2 and not last:
                                stage(0 if is_rest(g) else g + 1, s - 1)
                        if b < G and s < 2 and not last:
                            for k in range(RING + 2 * s, min(RING + 2 * s + 2, NLINES)):
                                line(n0 + b, k, (npar + b) % 2, own=False)
                        if work:
                            inter_hi(*work)
                    if b > 0 and not last:
                        evac_wd(n0 + b - 1, npar, b - 1)
                    if b < G - 1 and not last:
                        some_lines(n0 + b + 1, (npar + b + 1) % 2, range(RING), own=False)

            act.wait_ge(ga_out, 32 * (CHUNKS + 1))
            act.wait_ge(bx_split, NT)
            act.wait_ge(x1_out, 16 * NT)
            stage(REST, 0)
            for k in range(1, G):
                stage(0, k)
            evac_wd(REST_U, 1, 0)
            silu(REST, 0, 0)
            inter_hi(REST, 0, 0)
            group(REST, 1)
            with act.Fori(0, GROUPS // 2) as j:
                group(2 * j, 0)
                group(2 * j + 1, 1)
            group(GROUPS - 1, 0, last=True)

        @block.vector
        def _(dve):
            for k, (_, at_mid) in enumerate(LINES):
                dve.memset(line_c[:, k:k + 1], at_mid).then_inc(line_c_ready, 1)
            dve.memset(cond_bd[:, :, :], 0.0).then_inc(bd_zeroed, 1)
            dve.wait_ge(lora_in, 16 * 3)
            dve.tensor_scalar(lw[:, :], lw[:, :], LORA_SCALE, None, ALU.mult).then_inc(lw_ready, 1)
            dve.wait_ge(lw_ready, 1)
            lb_n = lb[:, :, :, :].rearrange("p n q r -> p n (q r)")
            dve.tensor_tensor(lb_n, lb_n, lw[:, :].unsqueeze(2).to_broadcast([P, NAD, P]), ALU.mult
                              ).then_inc(lw_ready, 1)
            dve.wait_ge(lw_ready, 2)
            dve.tensor_copy(lbq, lb[:, :, :, :].rearrange("p n q r -> p q n r")).then_inc(lb_scaled, 1)
            dve.wait_ge(ad_a_in, 16)
            dve.tensor_copy(ad_at[:, :, :, :], ad_araw.rearrange("p n q r -> p q n r")).then_inc(ad_at_ready, 1)
            dve.wait_ge(part_ready, 1)
            dve.tensor_scalar(part_ad[:, :], part_i[:, :], RANK.bit_length() - 1, None, ALU.logical_shift_right
                              ).then_inc(mask_step, 1)
            dve.wait_ge(mask_step, 1)
            dve.tensor_copy(part_f[:, :], part_ad[:, :]).then_inc(mask_step, 1)
            dve.wait_ge(mask_step, 2)
            dve.wait_ge(ad_ids_in, 16)
            dve.tensor_scalar(mask[:, :], ad_ids[:, :], part_f[:, 0:1], None, ALU.is_equal
                              ).then_inc(mask_step, 1)
            for jc in range(DC):
                dve.wait_ge(we_hi_ready, jc + 1)
                dve.tensor_tensor(we_lo[:, jc, :].rearrange("j (p q) -> j q p", q=DC),
                                  ps_o[1 - jc % 2][:, :].rearrange("j (q p) -> j q p", q=DC),
                                  we_hi[:, jc, :].bitcast(F32).rearrange("j (p q) -> j q p", q=DC),
                                  ALU.subtract).then_inc(we_lo_ready, 1)

            def combine(n, par, slot, ops, own=True):
                up, low = val_slot(slot), lower[:, par, :]
                for op in ops:
                    if op == 0:
                        dve.wait_ge(shifted, n + 1)
                        wait(dve, t_done, n - 2 if own else n - 1)
                        slope, at_mid = UPPER[0]
                        ins = dve.tensor_scalar(up, codes_slot(slot), slope, at_mid, ALU.mult, ALU.add)
                    else:
                        k = TAKEN_BY.index(op)
                        dve.wait_ge(lines, NLINES * n + k + (2 if op == 2 else 1))
                        if op == 2:
                            wait(dve, summed, n - 1)
                        else:
                            dve.wait_ge(combo, COMBOS * n + (1 if op == 1 else op - 1))
                        line = line_slot(k, own)
                        if op == 1:
                            ins = dve.scalar_tensor_tensor(out=up, in0=up, scalar=0.0, in1=line,
                                                           op0=ALU.max, op1=ALU.max)
                        elif op == 2:
                            ins = dve.scalar_tensor_tensor(out=low, in0=line, scalar=0.0, in1=line_slot(k + 1, own),
                                                           op0=ALU.min, op1=ALU.min)
                        elif op % 2 == 1:
                            ins = dve.tensor_tensor(up, up, line, ALU.max)
                        else:
                            ins = dve.tensor_tensor(low, low, line, ALU.min)
                    ins.then_inc(combo, 1)

            def low_y(tile):
                dve.wait_ge(y_hi_ready, tile + 1)
                dve.tensor_tensor(y_lo[:, :, :].rearrange("p q t -> p (q t)"), ps_y[:, :],
                                  y_hi[:, :, :].bitcast(F32).rearrange("p q t -> p (q t)"), ALU.subtract
                                  ).then_inc(y_lo_ready, 1)

            def sum_x1(tile):
                dve.wait_ge(z_mm, tile + 1)
                dve.wait_ge(xb_ready, tile + 1)
                dve.tensor_tensor(x1s[:, :], ps_z[:, :], x1s[:, :], ALU.add).then_inc(x1_ready, 1)

            def mask_bx(tile):
                dve.wait_ge(bx_mm, tile + 1)
                wait(dve, bx_split, tile)
                dve.tensor_tensor(bx_f.rearrange("p (s c) -> p s c", c=CH),
                                  ps_u[:, 0:P].rearrange("p (s c) -> p s c", c=CH),
                                  mask[:, ds(PER * tile, PER)].unsqueeze(2).to_broadcast([P, PER, CH]), ALU.mult
                                  ).then_inc(bx_masked, 1)

            def iteration(i, first=False):
                for s in range(UPI):
                    n, par, tile = UPI * i + s, s % 2, 2 * i + s // 3
                    combine(n, par, s % 3, (0, 1))
                    if s == 3 or (s == 0 and not first):
                        low_y(tile)
                    combine(n, par, s % 3, range(2, 6))
                    if s == 4 or (s == 1 and not first):
                        mask_bx(tile - 1)
                    if s % 3 == 2:
                        sum_x1(tile)
                    combine(n, par, s % 3, (6,))

            dve.wait_ge(mask_step, 3)
            low_y(0)
            iteration(0, first=True)
            with dve.Fori(1, ITER_A) as i:
                iteration(i)
            combine(TAIL_U, 0, 0, (0, 1))
            low_y(NT - 2)
            combine(TAIL_U, 0, 0, range(2, COMBOS))
            combine(REST_U, 1, 1, (0, 1))
            mask_bx(NT - 3)
            combine(REST_U, 1, 1, range(2, COMBOS))
            sum_x1(NT - 2)
            low_y(NT - 1)
            mask_bx(NT - 2)
            sum_x1(NT - 1)
            mask_bx(NT - 1)

            def product(g, b, k):
                q, rows, slot = chunk_no(g, b, k), REM if is_rest(g) else P, chunk_slot(g, b, k)
                dve.wait_ge(silu_ready, q + 1)
                dve.tensor_tensor(inter[0:rows, slot, :], ps_u[0:rows, :], inter[0:rows, slot, :], ALU.mult
                                  ).then_inc(inter_ready, 1)

            def product_low(g, b, k):
                q, rows, slot = chunk_no(g, b, k), REM if is_rest(g) else P, chunk_slot(g, b, k)
                dve.wait_ge(in_hi_ready, q + 1)
                dve.tensor_tensor(in_lo[0:rows, b % 2, k, :], inter[0:rows, slot, :],
                                  in_hi[0:rows, b % 2, k, :].bitcast(F32), ALU.subtract).then_inc(in_lo_ready, 1)

            def low_wd(n, gpar, k):
                dve.wait_ge(wd_hi_ready, n - REST_U + 1)
                dve.tensor_tensor(wd_lo[:, gpar, k, :], ps_t[:, :], wd_hi[:, gpar, k, :].bitcast(F32), ALU.subtract
                                  ).then_inc(wd_lo_ready, 1)

            def accumulate(g, t):
                r = t if is_rest(g) else NT * (g + 1) + t
                if is_rest(g) and t % TPB == 0:
                    dve.wait_ge(acc_in[t // TPB], 16)
                dve.wait_ge(down_mm, r + 1)
                dve.tensor_tensor(acc[:, t, :], ps_o[t % 2][:, :], acc[:, t, :], ALU.add).then_inc(added, 1)

            def group(g, gpar, last=False):
                n0, npar = next_units(g), 1 - gpar
                for b in range(NB):
                    for s, ops in enumerate(((0, 1, 2), (3, 4), (5,), (6,))):
                        work = next_chunk(g, b, s - 1, last)
                        if work:
                            product(*work)
                        if b < G and not last:
                            combine(n0 + b, (npar + b) % 2, (npar + b) % 2, ops, own=False)
                        if work:
                            product_low(*work)
                        if s == TPB - 1 and b > 0 and not last:
                            low_wd(n0 + b - 1, npar, b - 1)
                        accumulate(g, TPB * b + s)

            low_wd(REST_U, 1, 0)
            product(REST, 0, 0)
            product_low(REST, 0, 0)
            group(REST, 1)
            with dve.Fori(0, GROUPS // 2) as j:
                group(2 * j, 0)
                group(2 * j + 1, 1)
            group(GROUPS - 1, 0, last=True)

        @block.tensor
        def _(pe):
            pe.wait_ge(ident_ready, 2)
            pe.wait_ge(lb_scaled, 1)
            for q in range(DC):
                ins = pe.transpose(ps_t[:, q * P:(q + 1) * P], lbq[:, q, :, :].rearrange("p n r -> p (n r)"), ident[:, :])
            ins.then_inc(setup_t, 1)
            pe.wait_ge(ad_b_in, 16)
            for q in range(DC):
                ins = pe.transpose(ps_y[:, q * P:(q + 1) * P], val[:, 1, q * P:(q + 1) * P], ident[:, :])
            ins.then_inc(setup_t, 1)
            pe.wait_ge(setup_evac, 1)
            for jc in range(DC):
                if jc == 1:
                    pe.wait_ge(setup_evac, 2)
                if jc >= 2:
                    pe.wait_ge(we_lo_ready, jc - 1)
                ps = ps_o[1 - jc % 2]
                for h in range(2):
                    pe.matmul(ps[:, h * HALF:(h + 1) * HALF], la[:, jc * P:(jc + 1) * P],
                              ring_more[:, 0, h * HALF:(h + 1) * HALF], start=True, stop=False)
                pe.wait_ge(w_in[jc % 2], 16 * (jc // 2 + 1))
                for q in range(DC):
                    ins = pe.matmul(ps[:, q * P:(q + 1) * P], w_chunk[jc % 2][:, q, :], ident[:, :],
                                    start=False, stop=q % 4 == 3)
                ins.then_inc(we_mm, 1)

            def cond_y(tile, slot, loads):
                pe.wait_ge(x_in[slot], 16 * loads)
                wait(pe, y_lo_ready, tile)
                for jc in range(DC):
                    ins = pe.matmul(ps_y[:, jc * P:(jc + 1) * P], xs[:, slot, jc * P:(jc + 1) * P],
                                    cond_bd[:, ds(tile, 1), :].rearrange("p a n -> p (a n)"),
                                    start=True, stop=True)
                ins.then_inc(y_mm, 1)

            def ffn_z(tile, part):
                if part == 0:
                    pe.wait_ge(y_lo_ready, tile + 1)
                    wait(pe, x1t_ready, tile)
                for jc in range(part * DC // 2, (part + 1) * DC // 2):
                    for p, (y, w) in enumerate(((y_hi, we_hi), (y_hi, we_lo), (y_lo, we_hi))):
                        for h in range(2):
                            ins = pe.matmul(ps_z[:, h * HALF:(h + 1) * HALF], y[:, jc, :],
                                            w[:, jc, h * HALF:(h + 1) * HALF],
                                            start=jc == 0 and p == 0, stop=jc == DC - 1 and p == 2)
                if part == 1:
                    ins.then_inc(z_mm, 1)

            def turn_x1(tile):
                pe.wait_ge(x1_ready, tile + 1)
                for q in range(DC):
                    ins = pe.transpose(ps_z[:, q * P:(q + 1) * P], x1s[:, q * P:(q + 1) * P], ident[:, :])
                ins.then_inc(x1t_mm, 1)

            def adapter_bx(tile):
                pe.wait_ge(x1t_ready, tile + 1)
                wait(pe, bx_masked, tile)
                for q in range(DC):
                    ins = pe.matmul(ps_u[:, 0:P], ad_bt[:, q, :], x1t[:, q, :], start=q == 0, stop=q == DC - 1)
                ins.then_inc(bx_mm, 1)

            def turn_unit(n, slot):
                pe.wait_ge(scaled, n + 1)
                wait(pe, wt_ready, n)
                v = val_slot(slot).rearrange("i (p q) -> i q p", q=DC)
                for q in range(DC):
                    ins = pe.transpose(ps_t[:, q * P:(q + 1) * P], v[:, q, :], ident[:, :])
                ins.then_inc(t_done, 1)

            def adapter_ga(n, par, chunk):
                pe.wait_ge(wt_ready, n + 1)
                if par == 0:
                    wait(pe, ga_evac, chunk)
                for q in range(DC):
                    ins = pe.matmul(ps_g[:, par * P:(par + 1) * P], ad_at[:, q, :, :].rearrange("p n r -> p (n r)"), wt[:, par, q, :],
                                    start=q == 0, stop=q == DC - 1)
                ins.then_inc(ga_mm, 1)

            def iteration(i, first=False):
                for s in range(UPI):
                    n, par, tile, part = UPI * i + s, s % 2, 2 * i + s // 3, s % 3
                    if s > 1 or not first:
                        adapter_ga(n - 2, par, G * i + s // 2 - 1)
                    if s > 0 or not first:
                        turn_unit(n - 1, (s - 1) % 3)
                    if part < 2:
                        ffn_z(tile, part)
                    if part == 0 and (s > 0 or not first):
                        adapter_bx(tile - 1)
                    if part == 1:
                        cond_y(tile + 1, 1 - s // 3, i + 1 + s // 3)
                    if part == 2:
                        turn_x1(tile)

            pe.wait_ge(bd_in, 16 * SAMPLES)
            pe.wait_ge(we_lo_ready, DC)
            cond_y(0, 0, 1)
            pe.wait_ge(ad_at_ready, 1)
            iteration(0, first=True)
            with pe.Fori(1, ITER_A) as i:
                iteration(i)
            adapter_ga(TAIL_U - 2, 0, CHUNKS - 1)
            ffn_z(NT - 2, 0)
            turn_unit(TAIL_U - 1, 2)
            adapter_bx(NT - 3)
            adapter_ga(TAIL_U - 1, 1, CHUNKS - 1)
            ffn_z(NT - 2, 1)
            turn_unit(TAIL_U, 0)
            cond_y(NT - 1, 1, NT // 2)
            adapter_ga(TAIL_U, 0, CHUNKS)
            turn_x1(NT - 2)
            ffn_z(NT - 1, 0)
            adapter_bx(NT - 2)
            ffn_z(NT - 1, 1)
            turn_x1(NT - 1)
            adapter_bx(NT - 1)

            def turn_down(n, par):
                pe.wait_ge(scaled, n + 1)
                wait(pe, wd_lo_ready, n - REST_U)
                for t in range(DC):
                    ins = pe.transpose(ps_t[:, t * P:(t + 1) * P], val[:, par, t * P:(t + 1) * P], ident[:, :])
                ins.then_inc(t_done, 1)

            def gate_up(g, b, k):
                q = chunk_no(g, b, k)
                if b == 0:
                    loads = 1 if is_rest(g) else g + 1 + (k == 0)
                    pe.wait_ge(stage_in[k], 32 * loads)
                wait(pe, silu_ready, q)
                wait(pe, inter_ready, q)
                cols = slice(b * HALF, (b + 1) * HALF)
                for m, ps in enumerate((ps_g, ps_u)):
                    for p, (w, v) in enumerate(((st_hi, bx_hi), (st_hi, bx_lo), (st_lo, bx_hi))):
                        ins = pe.matmul(ps[:, :], w[:, k, m, :], v[:, cols], start=p == 0, stop=p == 2)
                ins.then_inc(gu_mm, 1)

            def down(g, b, s, gpar):
                chunks, rows = (1, REM) if is_rest(g) else (G, P)
                t = TPB * b + s
                if s == 0:
                    pe.wait_ge(in_lo_ready, chunk_no(g, b, chunks - 1) + 1)
                if s == 0 and b == 0:
                    pe.wait_ge(wd_lo_ready, 1 if is_rest(g) else 1 + G * (g + 1))
                wait(pe, added, (t if is_rest(g) else NT * (g + 1) + t) - 1)
                for k in range(chunks):
                    for p, (v, w) in enumerate(((in_hi, wd_hi), (in_hi, wd_lo), (in_lo, wd_hi))):
                        for h in range(2):
                            ins = pe.matmul(ps_o[t % 2][:, h * HALF:(h + 1) * HALF],
                                            v[0:rows, b % 2, k, s * P:(s + 1) * P],
                                            w[0:rows, gpar, k, h * HALF:(h + 1) * HALF],
                                            start=k == 0 and p == 0, stop=k == chunks - 1 and p == 2)
                ins.then_inc(down_mm, 1)

            def group(g, gpar, last=False):
                n0, npar = next_units(g), 1 - gpar
                for b in range(NB):
                    for s in range(TPB):
                        down(g, b, s, gpar)
                        work = next_chunk(g, b, s, last)
                        if work:
                            gate_up(*work)
                        if s == 1 and b > 0 and not last:
                            turn_down(n0 + b - 1, (npar + b - 1) % 2)

            pe.wait_ge(wt_ready, REST_U)
            turn_down(REST_U, 1)
            pe.wait_ge(ga_evac, CHUNKS + 1)
            pe.wait_ge(bx_split, NT)
            gate_up(REST, 0, 0)
            group(REST, 1)
            with pe.Fori(0, GROUPS // 2) as j:
                group(2 * j, 0)
                group(2 * j + 1, 1)
            group(GROUPS - 1, 0, last=True)


_INS = ["x", "itok_B_0_15", "itok_B_3_7", "L0_cond_weights", "L0_ffn_lora_A", "L0_ffn_lora_B", "L0_ffn_W",
        "L0_ffn_bias", "L0_ffn_lora_weights", "L1_cond_A", "L1_cond_B", "L1_ffn_gate_codes",
        "L1_ffn_gate_scales", "L1_ffn_up_codes", "L1_ffn_up_scales", "L1_ffn_down_codes", "L1_ffn_down_scales"]


def kernel(**inputs):
    import numpy as _np
    import concourse.bacc as _bacc
    from concourse import mybir as _mybir
    from concourse.bass_utils import run_bass_kernel_spmd as _run

    nc = _bacc.Bacc("TRN2", target_bir_lowering=False, num_devices=1)
    arrays, args = {}, []
    for name in _INS:
        a = _np.ascontiguousarray(inputs[name])
        arrays[f"in_{name}"] = a
        args.append(nc.dram_tensor(f"in_{name}", a.shape, _mybir.dt.from_np(a.dtype), kind="ExternalInput").ap())
    shape = inputs["x"].shape
    out = nc.dram_tensor("out", shape, _mybir.dt.float32, kind="ExternalOutput").ap()
    adaln_ffn(nc, *args, out)
    r = _run(nc, [arrays], core_ids=[0])
    return r.results[0]["out"]
```

```python
from contextlib import ExitStack

import numpy as np

import concourse.bass as bass
from concourse import mybir

F32 = mybir.dt.float32
F32R = mybir.dt.float32r
I32 = mybir.dt.int32
ALU = mybir.AluOpType
ACT = mybir.ActivationFunctionType
ds = bass.ds

NF4 = [-1.0, -0.6961928009986877, -0.5250730514526367, -0.39491748809814453, -0.28444138169288635,
       -0.18477343022833234, -0.09105003625154495, 0.0, 0.07958029955625534, 0.16093020141124725,
       0.24611230194568634, 0.33791524171829224, 0.44070982933044434, 0.5626170039176941,
       0.7229568362236023, 1.0]
MID = 8
UPPER = [(0.08134990185499191, 0.07958029955625534), (0.0918029248714447, 0.06250645220279694),
         (0.12190713733434677, -0.046918708831071854), (0.2770431339740753, -0.9393019676208496)]
LOWER = [(0.09105003625154495, 0.09105003625154495), (0.09966794401407242, 0.11423040181398392),
         (0.1301555186510086, 0.2558600902557373), (0.30380719900131226, 1.430457592010498)]
LINES = [UPPER[1], LOWER[0], LOWER[1], UPPER[2], LOWER[2], UPPER[3], LOWER[3]]
NLINES = len(LINES)
TAKEN_BY = [1, 2, 2, 3, 4, 5, 6]
COMBOS = 7


def check_lines():
    for code, level in enumerate(NF4):
        at = [np.float32(np.float64(code - MID) * m + c) for m, c in UPPER + LOWER]
        at[0] = np.float32(np.float32(code - MID) * np.float32(UPPER[0][0])) + np.float32(UPPER[0][1])
        up, low = max(0.0, *at[:4]), min(0.0, *at[4:])
        assert np.float32(up + low) == np.float32(level)


def adaln_ffn(nc, x, cond_id, adapter_id, cond_w, lora_a, lora_b, w0, bias0, lora_w, ad_a, ad_b,
              gate_codes, gate_scales, up_codes, up_scales, down_codes, down_scales, out):
    check_lines()
    SAMPLES, CH, D = x.shape
    P = 128
    ROWS = SAMPLES * CH
    NT = ROWS // P
    PER = P // CH
    DC = D // P
    HALF = 512
    NCOND = cond_w.shape[0]
    NAD, RANK, _ = ad_b.shape
    NR = NAD * RANK
    LORA_SCALE = 32 / lora_a.shape[1]
    HID = gate_codes.shape[0]
    BLK = D // gate_scales.shape[1]
    SB = gate_scales.shape[1]
    DSB = down_scales.shape[1]
    CHUNKS = HID // P
    REM = HID - CHUNKS * P
    G = 3
    GROUPS = CHUNKS // G
    NB = ROWS // HALF
    TPB = HALF // P
    ITER_A = 7
    UPI = 2 * CHUNKS // ITER_A
    TAIL_U = 2 * CHUNKS
    DOWN_U = TAIL_U + 1
    assert NR == P and 2 * REM == P and GROUPS * G == CHUNKS and ITER_A * UPI == TAIL_U
    assert UPI == 6 and NT == 2 * ITER_A + 2 and GROUPS % 2 == 1 and BLK == 64 and RANK == 16
    RING = 4

    x_rows = x.rearrange("s c d -> (s c) d")
    out_rows = out.rearrange("s c d -> (s c) d")
    x1_dram = nc.dram_tensor("x1_scratch", [ROWS, D], F32, kind="Internal").ap()
    ga_hi_dram = nc.dram_tensor("ga_hi_scratch", [CHUNKS + 1, P, 2 * P], F32, kind="Internal").ap()
    ga_lo_dram = nc.dram_tensor("ga_lo_scratch", [CHUNKS + 1, P, 2 * P], F32, kind="Internal").ap()

    with ExitStack() as ctx:
        def sb(name, shape, dt, where=ctx):
            return where.enter_context(nc.sbuf_tensor(name, shape, dt))

        def sem(name):
            return ctx.enter_context(nc.semaphore(name))

        ident = sb("ident", [P, P], F32)
        mid = sb("mid", [P, 1], I32)
        one = sb("one", [P, 1], F32)
        d_scales = sb("d_scales", [P, DC, DSB], F32)
        mask = sb("mask", [P, SAMPLES], F32)
        bx_hi = sb("bx_hi", [P, ROWS], F32R)
        bx_lo = sb("bx_lo", [P, ROWS], F32R)
        codes = sb("codes", [P, 2, D], I32)
        ring = sb("ring", [P, RING, D], F32)
        lower = sb("lower", [P, 2, D], F32)
        val = sb("val", [P, 2, D], F32)

        phase_a = ExitStack()
        we_hi = sb("we_hi", [P, DC, D], F32R, phase_a)
        we_lo = sb("we_lo", [P, DC, D], F32R, phase_a)
        cond_bd = sb("cond_bd", [P, NT, P], F32, phase_a)
        ring_more = sb("ring_more", [P, NLINES - RING, D], F32, phase_a)
        val_more = sb("val_more", [P, D], F32, phase_a)
        codes_more = sb("codes_more", [P, D], I32, phase_a)
        ad_at = sb("ad_at", [P, DC, NAD, RANK], F32, phase_a)
        wt = sb("wt", [P, 2, DC, P], F32, phase_a)
        xs = sb("xs", [P, 2, D], F32, phase_a)
        y_hi = sb("y_hi", [P, DC, P], F32R, phase_a)
        y_lo = sb("y_lo", [P, DC, P], F32R, phase_a)
        x1s = sb("x1s", [P, D], F32, phase_a)
        x1t = sb("x1t", [P, DC, P], F32, phase_a)
        ad_bt = sb("ad_bt", [P, DC, P], F32, phase_a)
        bias_b = sb("bias_b", [P, D], F32, phase_a)
        ga_hi = sb("ga_hi", [P, 2 * P], F32R, phase_a)
        ga_lo = sb("ga_lo", [P, 2 * P], F32R, phase_a)
        la = sb("la", [P, D], F32, phase_a)
        lb = sb("lb", [P, NAD, DC, RANK], F32, phase_a)
        gu_scales = sb("gu_scales", [P, CHUNKS + 1, 2, SB], F32, phase_a)
        lw = sb("lw", [P, NAD], F32, phase_a)
        cond_ids = sb("cond_ids", [1, SAMPLES], I32, phase_a)
        ad_ids = sb("ad_ids", [P, SAMPLES], I32, phase_a)
        part_i = sb("part_i", [P, 1], I32, phase_a)
        part_ad = sb("part_ad", [P, 1], I32, phase_a)
        part_f = sb("part_f", [P, 1], F32, phase_a)
        lbt = val_more[:, :]
        ad_braw = val[:, 1, :]
        ad_araw = ring[:, 1, :].rearrange("p (n q r) -> p n q r", n=NAD, q=DC)
        lbq = ring[:, 0, :].rearrange("p (q n r) -> p q n r", n=NAD, q=DC)
        ga_f = la[:, 0:2 * P]
        bx_f = la[:, 2 * P:3 * P]
        w_chunk = [x1s[:, :].rearrange("p (q j) -> p q j", q=DC), x1t[:, :, :]]
        phase_a.close()

        acc = sb("acc", [P, NT, D], F32)
        st_hi = sb("st_hi", [P, G + 1, 2, P], F32R)
        st_lo = sb("st_lo", [P, G + 1, 2, P], F32R)
        wd_hi = sb("wd_hi", [P, 2, G, D], F32R)
        wd_lo = sb("wd_lo", [P, 2, G, D], F32R)
        in_hi = sb("in_hi", [P, 2, G, HALF], F32R)
        in_lo = sb("in_lo", [P, 2, G, HALF], F32R)
        inter = sb("inter", [P, 2, HALF], F32)

        ps_y = ctx.enter_context(nc.psum_tensor("ps_y", [P, D], F32))
        ps_z = ctx.enter_context(nc.psum_tensor("ps_z", [P, D], F32))
        ps_t = ctx.enter_context(nc.psum_tensor("ps_t", [P, D], F32))
        ps_g = ctx.enter_context(nc.psum_tensor("ps_g", [P, HALF], F32))
        ps_u = ctx.enter_context(nc.psum_tensor("ps_u", [P, HALF], F32))
        ps_o = [ps_y, ps_z]

        ids_in = sem("ids_in")
        ad_ids_in = sem("ad_ids_in")
        lora_in = sem("lora_in")
        ad_b_in = sem("ad_b_in")
        ad_a_in = sem("ad_a_in")
        bias_in = sem("bias_in")
        scales_in = sem("scales_in")
        bd_first_in = sem("bd_first_in")
        bd_in = [sem(f"bd_in{k}") for k in range(PER)]
        w_in = [sem(f"w_in{k}") for k in range(2)]
        x_in = [sem(f"x_in{k}") for k in range(2)]
        codes_in = [sem(f"codes_in{k}") for k in range(3)]
        down_codes_in = [sem(f"down_codes_in{k}") for k in range(2)]
        stage_in = [sem(f"stage_in{k}") for k in range(G + 1)]
        acc_in = [sem(f"acc_in{k}") for k in range(NB)]
        x1_out = sem("x1_out")
        ga_out = sem("ga_out")
        out_done = sem("out_done")
        consts_ready = sem("consts_ready")
        ident_ready = sem("ident_ready")
        bd_zeroed = sem("bd_zeroed")
        part_ready = sem("part_ready")
        mask_step = sem("mask_step")
        lw_ready = sem("lw_ready")
        ad_at_ready = sem("ad_at_ready")
        lb_scaled = sem("lb_scaled")
        setup_t = sem("setup_t")
        setup_evac = sem("setup_evac")
        we_mm = sem("we_mm")
        we_hi_ready = sem("we_hi_ready")
        we_lo_ready = sem("we_lo_ready")
        shifted = sem("shifted")
        lines = sem("lines")
        combo = sem("combo")
        summed = sem("summed")
        scaled = sem("scaled")
        t_done = sem("t_done")
        wt_ready = sem("wt_ready")
        ga_mm = sem("ga_mm")
        ga_evac = sem("ga_evac")
        ga_step = sem("ga_step")
        ga_split = sem("ga_split")
        y_mm = sem("y_mm")
        y_hi_ready = sem("y_hi_ready")
        y_lo_ready = sem("y_lo_ready")
        z_mm = sem("z_mm")
        xb_ready = sem("xb_ready")
        x1_ready = sem("x1_ready")
        x1t_mm = sem("x1t_mm")
        x1t_ready = sem("x1t_ready")
        bx_mm = sem("bx_mm")
        bx_masked = sem("bx_masked")
        bx_step = sem("bx_step")
        bx_split = sem("bx_split")
        wd_hi_ready = sem("wd_hi_ready")
        wd_lo_ready = sem("wd_lo_ready")
        gu_mm = sem("gu_mm")
        silu_ready = sem("silu_ready")
        inter_ready = sem("inter_ready")
        in_hi_ready = sem("in_hi_ready")
        in_lo_ready = sem("in_lo_ready")
        down_mm = sem("down_mm")
        added = sem("added")

        LAST = GROUPS - 1

        def is_last(g):
            return isinstance(g, int) and g == LAST

        def chunks_of(g):
            return G + 1 if is_last(g) else G

        def rows_of(k):
            return REM if k == G else P

        def chunk_no(g, b, k):
            return NB * G * g + chunks_of(g) * b + k

        def chunk_slot(g, b, k):
            return (chunks_of(g) * b + k) % 2

        def next_chunk(g, b, k):
            if k < 0 or (b == NB - 1 and is_last(g)):
                return None
            then = (g, b + 1, k) if b < NB - 1 else (g + 1, 0, k)
            return then if k < chunks_of(then[0]) else None

        def next_unit(g, b):
            if is_last(g) or b < 0:
                return None
            return b if b < G or is_last(g + 1) else None

        def par_of(g, k):
            return (g + k) % 2

        def gate_up_banks(g, b, k):
            if b > 0 or not isinstance(g, int) or g > 0 or k == 0:
                return ps_g[:, :], ps_u[:, :]
            return ps_o[k % 2][:, 0:HALF], ps_o[k % 2][:, HALF:D]

        def half_slot(parts, more, b, k, rows):
            if k == G:
                return more[0:rows, 1, 1, (b % 2) * HALF:(b % 2 + 1) * HALF]
            return parts[0:rows, b % 2, k, :]

        def load_conds(eng, m, halves, signals):
            for half in halves:
                cid = eng.value_load(cond_ids[0:1, ds(PER * m + half, 1)], min_val=0, max_val=NCOND - 1)
                eng.dma_start(cond_bd[half * CH:(half + 1) * CH, ds(m, 1), half * CH:(half + 1) * CH],
                              cond_w[ds(cid, 1), :, :].rearrange("a c e -> c a e")).then_inc(signals[half], 16)

        def val_slot(n3):
            return val_more[:, :] if n3 == 2 else val[:, n3, :]

        def codes_slot(n3):
            return codes_more[:, :] if n3 == 2 else codes[:, n3, :]

        def line_slot(k, own):
            return ring_more[:, k - RING, :] if own and k >= RING else ring[:, k % RING, :]

        def wait(eng, semaphore, count):
            if not isinstance(count, int) or count > 0:
                eng.wait_ge(semaphore, count)

        block = ctx.enter_context(nc.Block())

        @block.sync
        def _(sp):
            def load_x(tile, slot):
                if not isinstance(tile, int) or tile > 1:
                    sp.wait_ge(y_mm, tile - 1)
                    sp.wait_ge(xb_ready, tile - 1)
                sp.dma_start(xs[:, slot, :], x_rows[ds(tile * P, P), :]).then_inc(x_in[slot], 16)

            def load_gu(n, slot, up, chunk):
                if not isinstance(n, int) or n > 2:
                    sp.wait_ge(lines, NLINES * (n - 2) + 1)
                sp.dma_start(codes_slot(slot), (up_codes if up else gate_codes)[ds(chunk * P, P), :]
                             ).then_inc(codes_in[slot], 16)

            def load_down(n, slot, col, width, count, signal):
                sp.wait_ge(lines, count)
                sp.dma_start(codes[:, slot, :].rearrange("p (t i) -> p t i", t=DC)[:, :, 0:width],
                             down_codes.rearrange("(t p) i -> p t i", p=P)[:, :, ds(col, width)]
                             ).then_inc(signal, 16)

            def load_down_chunk(c, behind_a=0, width=P):
                n, par = DOWN_U + c, 1 - c % 2 if isinstance(c, int) else None
                load_down(n, par, c * P, width, NLINES * (n - 1) + behind_a, down_codes_in[par])

            def store_x1(tile):
                sp.wait_ge(x1_ready, tile + 1)
                sp.dma_start(x1_dram[ds(tile * P, P), :], x1s[:, :]).then_inc(x1_out, 16)

            def store_ga(chunk):
                sp.wait_ge(ga_split, chunk + 1)
                for src, dst in ((ga_hi, ga_hi_dram), (ga_lo, ga_lo_dram)):
                    sp.dma_start(dst[ds(chunk, 1), :, :].rearrange("a p n -> p a n"),
                                 src[:, :].bitcast(F32).rearrange("p (a n) -> p a n", a=1)
                                 ).then_inc(ga_out, 16)

            load_gu(0, 0, 0, 0)
            sp.dma_start(cond_ids[:, :], cond_id.rearrange("(a s) -> a s", a=1)).then_inc(ids_in, 16)
            load_gu(1, 1, 1, 0)
            load_x(0, 0)
            load_gu(2, 2, 0, 1)
            sp.wait_ge(ids_in, 16)
            sp.wait_ge(bd_zeroed, 1)
            load_conds(sp, 0, range(PER), [bd_first_in] * PER)
            with sp.Fori(1, NT) as m:
                load_conds(sp, m, (0,), bd_in)
            load_x(1, 1)

            def iteration(i, first=False, last=False):
                for s in range(UPI):
                    n = UPI * i + s + 3
                    if not last or s < UPI // 2:
                        load_gu(n, s % 3, (s + 1) % 2, G * i + (s + 3) // 2)
                    elif s == UPI // 2:
                        sp.wait_ge(lines, NLINES * (n - 2) + 1)
                        for half, src in enumerate((gate_codes, up_codes)):
                            sp.dma_start(codes[half * REM:(half + 1) * REM, 0, :], src[CHUNKS * P:HID, :]
                                         ).then_inc(codes_in[0], 16)
                    elif s == UPI // 2 + 1:
                        load_down(n, 1, 0, P, NLINES * (n - 2) + 1, codes_in[1])
                    if s == 1 and not first:
                        store_ga(G * i - 1)
                    if s % 3 == 2:
                        load_x(2 * i + 2 + s // 3, s // 3)
                        store_x1(2 * i + s // 3)
                    if s == 3:
                        store_ga(G * i)
                    if s == 5:
                        store_ga(G * i + 1)

            iteration(0, first=True)
            with sp.Fori(1, ITER_A - 1) as i:
                iteration(i)
            iteration(ITER_A - 1, last=True)

            load_down_chunk(1, 1)
            store_ga(CHUNKS - 1)
            store_x1(NT - 2)
            store_ga(CHUNKS)
            load_down_chunk(2, 1)
            load_down_chunk(3)
            store_x1(NT - 1)
            sp.wait_ge(z_mm, NT)
            sp.wait_ge(x1_out, 16 * NT)
            for b in range(NB):
                sp.dma_start(acc[:, b * TPB:(b + 1) * TPB, :],
                             x1_dram[b * HALF:(b + 1) * HALF, :].rearrange("(t p) d -> p t d", p=P)
                             ).then_inc(acc_in[b], 16)
            load_down_chunk(4)
            with sp.Fori(2, CHUNKS // 2) as j:
                for par in range(2):
                    c = 2 * j + 1 + par
                    load_down(DOWN_U + c, par, c * P, P, NLINES * (DOWN_U + c - 1), down_codes_in[par])
            load_down_chunk(CHUNKS, 0, REM)
            for t in range(NT):
                sp.wait_ge(added, NT * LAST + t + 1)
                sp.dma_start(out_rows[t * P:(t + 1) * P, :], acc[:, t, :]).then_inc(out_done, 16)
            sp.wait_ge(out_done, 16 * NT)

        @block.gpsimd
        def _(pool):
            pool.memset(ident[:, :], 0.0).then_inc(ident_ready, 1)
            pool.wait_ge(ident_ready, 1)
            pool.affine_select(out=ident[:, :], in_=ident[:, :], compare_op=ALU.not_equal, fill=1.0, base=0,
                               pattern=[[-1, P]], channel_multiplier=1).then_inc(ident_ready, 1)
            pool.iota(part_i[:, :], pattern=[[0, 1]], base=0, channel_multiplier=1).then_inc(part_ready, 1)

            def shift(slot, signal, loads):
                pool.wait_ge(signal, 16 * loads)
                pool.tensor_tensor(codes_slot(slot), codes_slot(slot), mid[:, :].to_broadcast([P, D]), ALU.subtract
                                   ).then_inc(shifted, 1)

            def shift_down(par, loads):
                shift(par, down_codes_in[par], loads)

            def scale(n, par, slot, scales, blocks=None):
                v = val_slot(slot)
                pool.wait_ge(combo, COMBOS * (n + 1))
                pool.tensor_tensor(v, v, lower[:, par, :], ALU.add).then_inc(summed, 1)
                pool.wait_ge(summed, n + 1)
                b = v.rearrange("p (b j) -> p b j", j=BLK) if blocks is None else blocks(v)
                pool.tensor_tensor(b, b, scales, ALU.mult).then_inc(scaled, 1)

            def gu_scale(chunk, kind):
                return gu_scales[:, ds(chunk, 1), kind, :].rearrange("p a b -> p (a b)").unsqueeze(2
                                 ).to_broadcast([P, SB, BLK])

            def add_bias(tile, slot, i):
                pool.wait_ge(x_in[slot], 16 * (i + 1))
                wait(pool, x1_out, 16 * tile)
                wait(pool, x1t_mm, tile)
                pool.tensor_tensor(x1s[:, :], xs[:, slot, :], bias_b[:, :], ALU.add).then_inc(xb_ready, 1)

            def split_ga(chunk):
                pool.wait_ge(ga_evac, chunk + 1)
                wait(pool, ga_out, 32 * chunk)
                pool.tensor_tensor(ga_hi[:, :], ga_f, one[:, :].to_broadcast([P, 2 * P]), ALU.mult
                                   ).then_inc(ga_step, 1)
                pool.wait_ge(ga_step, chunk + 1)
                pool.tensor_tensor(ga_lo[:, :], ga_f, ga_hi[:, :].bitcast(F32), ALU.subtract
                                   ).then_inc(ga_split, 1)

            def split_bx(tile):
                hi, lo = bx_hi[:, ds(tile * P, P)], bx_lo[:, ds(tile * P, P)]
                pool.wait_ge(bx_masked, tile + 1)
                pool.tensor_tensor(hi, bx_f, one[:, :].to_broadcast([P, P]), ALU.mult
                                   ).then_inc(bx_step, 1)
                pool.wait_ge(bx_step, tile + 1)
                pool.tensor_tensor(lo, bx_f, hi.bitcast(F32), ALU.subtract).then_inc(bx_split, 1)

            def iteration(i, first=False, last=False):
                for s in range(UPI):
                    n, par = UPI * i + s, s % 2
                    if s % 3 == 1 and (s > 1 or not first):
                        add_bias(2 * i + s // 3, s // 3, i)
                    slot = (s + 2) % 3
                    shift(slot, codes_in[slot], 2 * i + (s + 2) // 3 + 1 + (last and s == UPI - 2))
                    if s == 5 or (s == 2 and not first):
                        split_bx(2 * i + s // 3 - 1)
                    if s % 2 == 1 and (s > 1 or not first):
                        split_ga(G * i + s // 2 - 1)
                    scale(n, par, s % 3, gu_scale(G * i + s // 2, par))
                    if first and s == 1:
                        pool.wait_ge(bias_in, 16)
                        pool.wait_ge(we_mm, DC)
                        add_bias(0, 0, 0)

            pool.memset(mid[:, :], MID).then_inc(consts_ready, 1)
            pool.memset(one[:, :], 1.0).then_inc(consts_ready, 1)
            pool.wait_ge(consts_ready, 2)
            shift(0, codes_in[0], 1)
            shift(1, codes_in[1], 1)
            pool.wait_ge(ids_in, 16)
            pool.wait_ge(bd_zeroed, 1)
            with pool.Fori(1, NT) as m:
                load_conds(pool, m, (1,), bd_in)
            pool.wait_ge(scales_in, 16 * 5)
            iteration(0, first=True)
            with pool.Fori(1, ITER_A - 1) as i:
                iteration(i)
            iteration(ITER_A - 1, last=True)

            def scale_down(c, par):
                scale(DOWN_U + c, par, par, d_scales[:, :, ds(2 * c, 2)].unsqueeze(3).to_broadcast([P, DC, 2, BLK]),
                      lambda v: v.rearrange("p (t b j) -> p t b j", t=DC, j=BLK))

            shift_down(0, 1)
            add_bias(NT - 2, 0, ITER_A)
            scale(TAIL_U, 0, 0, gu_scale(CHUNKS, 0))
            split_bx(NT - 3)
            split_ga(CHUNKS - 1)
            scale_down(0, 1)
            add_bias(NT - 1, 1, ITER_A)
            split_ga(CHUNKS)
            shift_down(1, 1)
            scale_down(1, 0)
            shift_down(0, 2)
            split_bx(NT - 2)
            scale_down(2, 1)
            split_bx(NT - 1)
            shift_down(1, 2)
            with pool.Fori(1, (CHUNKS - 3) // 2) as j:
                for par in range(2):
                    shift_down(par, j + 2)
                    scale_down(2 * j + 1 + par, par)
            shift_down(0, (CHUNKS + 1) // 2)
            scale_down(CHUNKS - 2, 0)
            scale_down(CHUNKS - 1, 1)
            scale(DOWN_U + CHUNKS, 0, 0, d_scales[:, :, DSB - 1:DSB].to_broadcast([P, DC, BLK]),
                  lambda v: v.rearrange("p (t j) -> p t j", t=DC)[:, :, 0:REM])

        @block.scalar
        def _(act):
            act.dma_start(lb[:, :, :, :].rearrange("p n q r -> p n (q r)"),
                          lora_b.rearrange("n (p q) r -> p n (q r)", p=P)).then_inc(lora_in, 16)
            act.dma_start(lw[:, :], lora_w.partition_broadcast(P)).then_inc(lora_in, 16)
            act.dma_start(la[:, :], lora_a.rearrange("n r d -> (n r) d")).then_inc(lora_in, 16)
            w_qj = w0.rearrange("(p q) j -> p q j", p=P)

            def load_w(jc):
                if jc >= 2:
                    act.wait_ge(we_mm, jc - 1)
                act.dma_start(w_chunk[jc % 2], w_qj[:, :, jc * P:(jc + 1) * P]).then_inc(w_in[jc % 2], 16)

            load_w(0)
            load_w(1)
            act.dma_start(ad_araw.rearrange("p n q r -> p n (q r)"),
                          ad_a.rearrange("n (p q) r -> p n (q r)", p=P)).then_inc(ad_a_in, 16)
            act.dma_start(ad_braw, ad_b.rearrange("n r d -> (n r) d")).then_inc(ad_b_in, 16)
            act.dma_start(ad_ids[:, :], adapter_id.partition_broadcast(P)).then_inc(ad_ids_in, 16)
            act.dma_start(bias_b[:, :], bias0.partition_broadcast(P)).then_inc(bias_in, 16)
            for kind, src in enumerate((gate_scales, up_scales)):
                act.dma_start(gu_scales[:, 0:CHUNKS, kind, :],
                              src[0:CHUNKS * P, :].rearrange("(c p) b -> p c b", p=P)).then_inc(scales_in, 16)
                act.dma_start(gu_scales[kind * REM:(kind + 1) * REM, CHUNKS, 0, :], src[CHUNKS * P:HID, :]
                              ).then_inc(scales_in, 16)
            act.dma_start(d_scales[:, :, :], down_scales.rearrange("(t p) b -> p t b", p=P)
                          ).then_inc(scales_in, 16)

            def line(n, k, slot, own=True):
                if k == 0:
                    act.wait_ge(shifted, n + 1)
                if own:
                    wait(act, combo, COMBOS * (n - 1) + TAKEN_BY[k] + 1)
                elif k >= RING:
                    act.wait_ge(combo, COMBOS * n + TAKEN_BY[k - RING] + 1)
                else:
                    before = max(j for j in range(NLINES) if j % RING == k)
                    act.wait_ge(combo, COMBOS * (n - 1) + TAKEN_BY[before] + 1)
                slope, at_mid = LINES[k]
                act.activation(line_slot(k, own), codes_slot(slot), ACT.Copy, bias=at_mid, scale=slope
                               ).then_inc(lines, 1)

            def some_lines(n, slot, ks, own=True):
                for k in ks:
                    line(n, k, slot, own)

            def evac_t(n, par):
                act.wait_ge(t_done, n + 1)
                wait(act, ga_mm, n - 1)
                act.activation(wt[:, par, :, :], ps_t[:, :].rearrange("p (q i) -> p q i", q=DC), ACT.Copy
                               ).then_inc(wt_ready, 1)

            def evac_y(tile):
                act.wait_ge(y_mm, tile + 1)
                wait(act, z_mm, tile)
                act.activation(y_hi[:, :, :].rearrange("p q t -> p (q t)"), ps_y[:, :], ACT.Copy
                               ).then_inc(y_hi_ready, 1)

            def evac_x1t(tile):
                act.wait_ge(x1t_mm, tile + 1)
                wait(act, bx_mm, tile)
                act.activation(x1t[:, :, :].rearrange("p q t -> p (q t)"), ps_z[:, :], ACT.Copy
                               ).then_inc(x1t_ready, 1)

            def evac_ga(chunk):
                act.wait_ge(ga_mm, 2 * chunk + 2)
                wait(act, ga_split, chunk)
                act.activation(ga_f, ps_g[:, 0:2 * P], ACT.Copy).then_inc(ga_evac, 1)

            act.wait_ge(setup_t, 1)
            act.activation(lbt, ps_t[:, :], ACT.Copy).then_inc(setup_evac, 1)
            act.wait_ge(ad_at_ready, 1)
            early = [(n, k) for n in range(3) for k in range(NLINES)]
            for jc in range(DC):
                for n, k in early[2 * jc:2 * jc + 2]:
                    line(n, k, n)
                if jc + 2 < DC:
                    load_w(jc + 2)
                act.wait_ge(we_mm, jc + 1)
                act.activation(we_hi[:, jc, :].rearrange("j (p q) -> j q p", q=DC),
                               ps_o[1 - jc % 2][:, :].rearrange("j (q p) -> j q p", q=DC), ACT.Copy
                               ).then_inc(we_hi_ready, 1)
                if jc == 2:
                    act.wait_ge(setup_t, 2)
                    act.activation(ad_bt[:, :, :].rearrange("p q t -> p (q t)"), ps_t[:, :], ACT.Copy
                                   ).then_inc(setup_evac, 1)
            evac_y(0)
            for n, k in early[2 * DC:]:
                line(n, k, n)

            def iteration(i, first=False):
                for s in range(1 if first else 0, UPI):
                    n, par, tile = UPI * i + s, s % 2, 2 * i + s // 3
                    if first and s == 1:
                        evac_t(0, 0)
                        continue
                    some_lines(n + 1, (s + 1) % 3, range(2))
                    if s == 3 or (s == 0 and not first):
                        evac_x1t(tile - 1)
                    some_lines(n + 1, (s + 1) % 3, range(2, 5))
                    if s % 2 == 1 and (s > 1 or not first):
                        evac_ga(G * i + s // 2 - 1)
                    if s % 3 == 2:
                        evac_y(tile + 1)
                    some_lines(n + 1, (s + 1) % 3, range(5, NLINES))
                    evac_t(n - 1, 1 - par)

            iteration(0, first=True)
            with act.Fori(1, ITER_A) as i:
                iteration(i)

            def stage(g, k):
                chunk = G * g + k
                for dst, src in ((st_hi, ga_hi_dram), (st_lo, ga_lo_dram)):
                    act.dma_start(dst[:, k:k + 1, :, :].bitcast(F32).rearrange("p a m i -> p a (m i)"),
                                  src[ds(chunk, 1), :, :].rearrange("a p n -> p a n")).then_inc(stage_in[k], 16)

            def silu(g, b, k):
                q, rows = chunk_no(g, b, k), rows_of(k)
                act.wait_ge(gu_mm, q + 1)
                wait(act, in_lo_ready, q - 1)
                act.activation(inter[0:rows, chunk_slot(g, b, k), :], gate_up_banks(g, b, k)[0][0:rows, :], ACT.Silu
                               ).then_inc(silu_ready, 1)

            def inter_hi(g, b, k):
                q, rows = chunk_no(g, b, k), rows_of(k)
                act.wait_ge(inter_ready, q + 1)
                act.activation(half_slot(in_hi, wd_hi, b, k, rows), inter[0:rows, chunk_slot(g, b, k), :], ACT.Copy
                               ).then_inc(in_hi_ready, 1)

            def evac_wd(n, gpar, k):
                act.wait_ge(t_done, n + 1)
                act.activation(wd_hi[:, gpar, k, :], ps_t[:, :], ACT.Copy).then_inc(wd_hi_ready, 1)

            some_lines(DOWN_U, 1, range(2))
            evac_x1t(NT - 3)
            some_lines(DOWN_U, 1, range(2, NLINES))
            evac_t(TAIL_U - 1, 1)
            evac_ga(CHUNKS - 1)
            some_lines(DOWN_U + 1, 0, range(2), own=False)
            evac_t(TAIL_U, 0)
            evac_y(NT - 1)
            some_lines(DOWN_U + 1, 0, range(2, RING), own=False)
            evac_x1t(NT - 2)
            act.wait_ge(ga_mm, TAIL_U + 1)
            act.wait_ge(ga_split, CHUNKS)
            act.activation(ga_f[:, 0:P], ps_g[:, 0:P], ACT.Copy)
            act.activation(ga_f[:, P:P + REM], ps_g[:, REM:P], ACT.Copy)
            act.activation(ga_f[:, P + REM:2 * P], ps_g[:, 0:REM], ACT.Copy).then_inc(ga_evac, 1)
            some_lines(DOWN_U + 1, 0, range(RING, NLINES), own=False)
            evac_wd(DOWN_U, 0, 0)
            some_lines(DOWN_U + 2, 1, range(RING), own=False)
            act.wait_ge(ga_out, 32 * (CHUNKS + 1))
            for k in range(G):
                stage(0, k)
            stage(LAST, G)
            some_lines(DOWN_U + 2, 1, range(RING, NLINES), own=False)
            evac_wd(DOWN_U + 1, 0, 1)
            evac_x1t(NT - 1)

            def group(g, gpar):
                n0 = DOWN_U + G * (g + 1)
                if is_last(g):
                    evac_wd(DOWN_U + CHUNKS, 1, 0)
                elif next_unit(g, 0) is not None:
                    some_lines(n0, par_of(gpar, 0), range(RING), own=False)
                for b in range(NB):
                    now, before, then = next_unit(g, b), next_unit(g, b - 1), next_unit(g, b + 1)
                    for s in range(TPB):
                        work = next_chunk(g, b, s - 1)
                        if work:
                            silu(*work)
                            if b == NB - 2 and s <= G and not is_last(g):
                                stage(g + 1, s - 1)
                        if now is not None and s < 2:
                            some_lines(n0 + now, par_of(gpar, now), range(RING + 2 * s, min(RING + 2 * s + 2, NLINES)),
                                       own=False)
                        if work:
                            inter_hi(*work)
                    if before is not None:
                        evac_wd(n0 + before, 1 - gpar, before)
                    if then is not None and b < NB - 1:
                        some_lines(n0 + then, par_of(gpar, then), range(RING), own=False)
                    work = next_chunk(g, b, G)
                    if work:
                        silu(*work)
                        inter_hi(*work)

            act.wait_ge(x1_out, 16 * NT)
            silu(0, 0, 0)
            silu(0, 0, 1)
            inter_hi(0, 0, 0)
            inter_hi(0, 0, 1)
            silu(0, 0, 2)
            evac_wd(DOWN_U + 2, 0, 2)
            inter_hi(0, 0, 2)
            with act.Fori(0, 2) as j:
                group(2 * j, 0)
                group(2 * j + 1, 1)
            for g in range(4, GROUPS):
                group(g, g % 2)

        @block.vector
        def _(dve):
            dve.memset(cond_bd[:, :, :], 0.0).then_inc(bd_zeroed, 1)
            dve.wait_ge(lora_in, 16 * 3)
            dve.tensor_scalar(lw[:, :], lw[:, :], LORA_SCALE, None, ALU.mult).then_inc(lw_ready, 1)
            dve.wait_ge(lw_ready, 1)
            lb_n = lb[:, :, :, :].rearrange("p n q r -> p n (q r)")
            dve.tensor_tensor(lb_n, lb_n, lw[:, :].unsqueeze(2).to_broadcast([P, NAD, P]), ALU.mult
                              ).then_inc(lw_ready, 1)
            dve.wait_ge(lw_ready, 2)
            dve.tensor_copy(lbq, lb[:, :, :, :].rearrange("p n q r -> p q n r")).then_inc(lb_scaled, 1)
            dve.wait_ge(ad_a_in, 16)
            dve.tensor_copy(ad_at[:, :, :, :], ad_araw.rearrange("p n q r -> p q n r")).then_inc(ad_at_ready, 1)
            dve.wait_ge(part_ready, 1)
            dve.tensor_scalar(part_ad[:, :], part_i[:, :], RANK.bit_length() - 1, None, ALU.logical_shift_right
                              ).then_inc(mask_step, 1)
            dve.wait_ge(mask_step, 1)
            dve.tensor_copy(part_f[:, :], part_ad[:, :]).then_inc(mask_step, 1)
            dve.wait_ge(mask_step, 2)
            dve.wait_ge(ad_ids_in, 16)
            dve.tensor_scalar(mask[:, :], ad_ids[:, :], part_f[:, 0:1], None, ALU.is_equal
                              ).then_inc(mask_step, 1)
            def combine(n, par, slot, ops, own=True):
                up, low = val_slot(slot), lower[:, par, :]
                for op in ops:
                    if op == 0:
                        dve.wait_ge(shifted, n + 1)
                        wait(dve, t_done, n - 2 if own else n - 1)
                        slope, at_mid = UPPER[0]
                        ins = dve.tensor_scalar(up, codes_slot(slot), slope, at_mid, ALU.mult, ALU.add)
                    else:
                        k = TAKEN_BY.index(op)
                        dve.wait_ge(lines, NLINES * n + k + (2 if op == 2 else 1))
                        if op == 2:
                            wait(dve, summed, n - 1)
                        else:
                            dve.wait_ge(combo, COMBOS * n + (1 if op == 1 else op - 1))
                        line = line_slot(k, own)
                        if op == 1:
                            ins = dve.scalar_tensor_tensor(out=up, in0=up, scalar=0.0, in1=line,
                                                           op0=ALU.max, op1=ALU.max)
                        elif op == 2:
                            ins = dve.scalar_tensor_tensor(out=low, in0=line, scalar=0.0, in1=line_slot(k + 1, own),
                                                           op0=ALU.min, op1=ALU.min)
                        elif op % 2 == 1:
                            ins = dve.tensor_tensor(up, up, line, ALU.max)
                        else:
                            ins = dve.tensor_tensor(low, low, line, ALU.min)
                    ins.then_inc(combo, 1)

            early = [(n, op) for n in range(2) for op in range(COMBOS)]
            for jc in range(DC):
                for n, op in early[2 * jc:2 * jc + 2]:
                    if (n, op) == (1, 0):
                        dve.wait_ge(setup_t, 2)
                    combine(n, n, n, (op,))
                dve.wait_ge(we_hi_ready, jc + 1)
                dve.tensor_tensor(we_lo[:, jc, :].rearrange("j (p q) -> j q p", q=DC),
                                  ps_o[1 - jc % 2][:, :].rearrange("j (q p) -> j q p", q=DC),
                                  we_hi[:, jc, :].bitcast(F32).rearrange("j (p q) -> j q p", q=DC),
                                  ALU.subtract).then_inc(we_lo_ready, 1)

            def low_y(tile):
                dve.wait_ge(y_hi_ready, tile + 1)
                dve.tensor_tensor(y_lo[:, :, :].rearrange("p q t -> p (q t)"), ps_y[:, :],
                                  y_hi[:, :, :].bitcast(F32).rearrange("p q t -> p (q t)"), ALU.subtract
                                  ).then_inc(y_lo_ready, 1)

            def sum_x1(tile):
                dve.wait_ge(z_mm, tile + 1)
                dve.wait_ge(xb_ready, tile + 1)
                dve.tensor_tensor(x1s[:, :], ps_z[:, :], x1s[:, :], ALU.add).then_inc(x1_ready, 1)

            def mask_bx(tile):
                dve.wait_ge(bx_mm, tile + 1)
                wait(dve, bx_split, tile)
                dve.tensor_tensor(bx_f.rearrange("p (s c) -> p s c", c=CH),
                                  ps_u[:, 0:P].rearrange("p (s c) -> p s c", c=CH),
                                  mask[:, ds(PER * tile, PER)].unsqueeze(2).to_broadcast([P, PER, CH]), ALU.mult
                                  ).then_inc(bx_masked, 1)

            def iteration(i, first=False):
                for s in range(2 if first else 0, UPI):
                    n, par, tile = UPI * i + s, s % 2, 2 * i + s // 3
                    combine(n, par, s % 3, (0, 1))
                    if s == 3 or (s == 0 and not first):
                        low_y(tile)
                    combine(n, par, s % 3, range(2, 6))
                    if s == 4 or (s == 1 and not first):
                        mask_bx(tile - 1)
                    if s % 3 == 2:
                        sum_x1(tile)
                    combine(n, par, s % 3, (6,))

            dve.wait_ge(mask_step, 3)
            low_y(0)
            iteration(0, first=True)
            with dve.Fori(1, ITER_A) as i:
                iteration(i)
            def product(g, b, k):
                q, rows, slot = chunk_no(g, b, k), rows_of(k), chunk_slot(g, b, k)
                dve.wait_ge(silu_ready, q + 1)
                dve.tensor_tensor(inter[0:rows, slot, :], gate_up_banks(g, b, k)[1][0:rows, :], inter[0:rows, slot, :], ALU.mult
                                  ).then_inc(inter_ready, 1)

            def product_low(g, b, k):
                q, rows, slot = chunk_no(g, b, k), rows_of(k), chunk_slot(g, b, k)
                dve.wait_ge(in_hi_ready, q + 1)
                dve.tensor_tensor(half_slot(in_lo, wd_lo, b, k, rows), inter[0:rows, slot, :],
                                  half_slot(in_hi, wd_hi, b, k, rows).bitcast(F32), ALU.subtract).then_inc(in_lo_ready, 1)

            def low_wd(n, gpar, k):
                dve.wait_ge(wd_hi_ready, n - DOWN_U + 1)
                dve.tensor_tensor(wd_lo[:, gpar, k, :], ps_t[:, :], wd_hi[:, gpar, k, :].bitcast(F32), ALU.subtract
                                  ).then_inc(wd_lo_ready, 1)

            combine(TAIL_U, 0, 0, (0, 1))
            low_y(NT - 2)
            combine(TAIL_U, 0, 0, range(2, COMBOS))
            combine(DOWN_U, 1, 1, (0, 1))
            combine(DOWN_U, 1, 1, range(2, 6))
            mask_bx(NT - 3)
            combine(DOWN_U, 1, 1, (6,))
            sum_x1(NT - 2)
            low_y(NT - 1)
            combine(DOWN_U + 1, 0, 0, range(4), own=False)
            mask_bx(NT - 2)
            combine(DOWN_U + 1, 0, 0, range(4, COMBOS), own=False)
            dve.wait_ge(xb_ready, NT)
            low_wd(DOWN_U, 0, 0)
            combine(DOWN_U + 2, 1, 1, range(3), own=False)
            sum_x1(NT - 1)
            combine(DOWN_U + 2, 1, 1, range(3, COMBOS), own=False)
            mask_bx(NT - 1)
            low_wd(DOWN_U + 1, 0, 1)

            def accumulate(g, t, first):
                r = NT * g + t
                if first and t % TPB == 0:
                    dve.wait_ge(acc_in[t // TPB], 16)
                dve.wait_ge(down_mm, r + 1)
                dve.tensor_tensor(acc[:, t, :], ps_o[t % 2][:, :], acc[:, t, :], ALU.add).then_inc(added, 1)

            def group(g, gpar, first=False):
                n0 = DOWN_U + G * (g + 1)
                if is_last(g):
                    low_wd(DOWN_U + CHUNKS, 1, 0)
                for b in range(NB):
                    now, before = next_unit(g, b), next_unit(g, b - 1)
                    for s, ops in enumerate(((0, 1, 2), (3, 4), (5,), (6,)) if b < G else
                                            ((0, 1, 2), (3, 4, 5, 6), (), ())):
                        work = next_chunk(g, b, s - 1)
                        if work:
                            product(*work)
                        if now is not None:
                            combine(n0 + now, par_of(gpar, now), par_of(gpar, now), ops, own=False)
                        if work:
                            product_low(*work)
                        if s == TPB - 1 and before is not None:
                            low_wd(n0 + before, 1 - gpar, before)
                        accumulate(g, TPB * b + s, first)
                    work = next_chunk(g, b, G)
                    if work:
                        product(*work)
                        product_low(*work)

            product(0, 0, 0)
            product(0, 0, 1)
            product_low(0, 0, 0)
            product_low(0, 0, 1)
            product(0, 0, 2)
            low_wd(DOWN_U + 2, 0, 2)
            product_low(0, 0, 2)
            group(0, 0, first=True)
            group(1, 1)
            with dve.Fori(1, 2) as j:
                group(2 * j, 0)
                group(2 * j + 1, 1)
            for g in range(4, GROUPS):
                group(g, g % 2)

        @block.tensor
        def _(pe):
            pe.wait_ge(ident_ready, 2)
            pe.wait_ge(lb_scaled, 1)
            for q in range(DC):
                ins = pe.transpose(ps_t[:, q * P:(q + 1) * P], lbq[:, q, :, :].rearrange("p n r -> p (n r)"), ident[:, :])
            ins.then_inc(setup_t, 1)
            pe.wait_ge(setup_evac, 1)
            for jc in range(DC):
                if jc >= 2:
                    pe.wait_ge(we_lo_ready, jc - 1)
                ps = ps_o[1 - jc % 2]
                for h in range(2):
                    pe.matmul(ps[:, h * HALF:(h + 1) * HALF], la[:, jc * P:(jc + 1) * P],
                              val_more[:, h * HALF:(h + 1) * HALF], start=True, stop=False)
                pe.wait_ge(w_in[jc % 2], 16 * (jc // 2 + 1))
                for q in range(DC):
                    ins = pe.matmul(ps[:, q * P:(q + 1) * P], w_chunk[jc % 2][:, q, :], ident[:, :],
                                    start=False, stop=q % 4 == 3)
                ins.then_inc(we_mm, 1)
                if jc == 1:
                    pe.wait_ge(ad_b_in, 16)
                    for q in range(DC):
                        ins = pe.transpose(ps_t[:, q * P:(q + 1) * P], val[:, 1, q * P:(q + 1) * P], ident[:, :])
                    ins.then_inc(setup_t, 1)

            def cond_y(tile, slot, loads):
                pe.wait_ge(x_in[slot], 16 * loads)
                wait(pe, y_lo_ready, tile)
                for jc in range(DC):
                    ins = pe.matmul(ps_y[:, jc * P:(jc + 1) * P], xs[:, slot, jc * P:(jc + 1) * P],
                                    cond_bd[:, ds(tile, 1), :].rearrange("p a n -> p (a n)"),
                                    start=True, stop=True)
                ins.then_inc(y_mm, 1)

            def ffn_z(tile, part):
                if part == 0:
                    pe.wait_ge(y_lo_ready, tile + 1)
                    wait(pe, x1t_ready, tile)
                for jc in range(part * DC // 2, (part + 1) * DC // 2):
                    for p, (y, w) in enumerate(((y_hi, we_hi), (y_hi, we_lo), (y_lo, we_hi))):
                        for h in range(2):
                            ins = pe.matmul(ps_z[:, h * HALF:(h + 1) * HALF], y[:, jc, :],
                                            w[:, jc, h * HALF:(h + 1) * HALF],
                                            start=jc == 0 and p == 0, stop=jc == DC - 1 and p == 2)
                if part == 1:
                    ins.then_inc(z_mm, 1)

            def turn_x1(tile):
                pe.wait_ge(x1_ready, tile + 1)
                for q in range(DC):
                    ins = pe.transpose(ps_z[:, q * P:(q + 1) * P], x1s[:, q * P:(q + 1) * P], ident[:, :])
                ins.then_inc(x1t_mm, 1)

            def adapter_bx(tile):
                pe.wait_ge(x1t_ready, tile + 1)
                wait(pe, bx_masked, tile)
                for q in range(DC):
                    ins = pe.matmul(ps_u[:, 0:P], ad_bt[:, q, :], x1t[:, q, :], start=q == 0, stop=q == DC - 1)
                ins.then_inc(bx_mm, 1)

            def turn_unit(n, slot):
                pe.wait_ge(scaled, n + 1)
                wait(pe, wt_ready, n)
                v = val_slot(slot).rearrange("i (p q) -> i q p", q=DC)
                for q in range(DC):
                    ins = pe.transpose(ps_t[:, q * P:(q + 1) * P], v[:, q, :], ident[:, :])
                ins.then_inc(t_done, 1)

            def adapter_ga(n, par, chunk):
                pe.wait_ge(wt_ready, n + 1)
                if par == 0:
                    wait(pe, ga_evac, chunk)
                for q in range(DC):
                    ins = pe.matmul(ps_g[:, par * P:(par + 1) * P], ad_at[:, q, :, :].rearrange("p n r -> p (n r)"), wt[:, par, q, :],
                                    start=q == 0, stop=q == DC - 1)
                ins.then_inc(ga_mm, 1)

            def iteration(i, first=False):
                for s in range(UPI):
                    n, par, tile, part = UPI * i + s, s % 2, 2 * i + s // 3, s % 3
                    if s > 1 or not first:
                        adapter_ga(n - 2, par, G * i + s // 2 - 1)
                    if s > 0 or not first:
                        turn_unit(n - 1, (s - 1) % 3)
                    if part < 2:
                        ffn_z(tile, part)
                    if part == 0 and (s > 0 or not first):
                        adapter_bx(tile - 1)
                    if part == 1:
                        cond_y(tile + 1, 1 - s // 3, i + 1 + s // 3)
                    if part == 2:
                        turn_x1(tile)

            pe.wait_ge(bd_first_in, 16 * PER)
            pe.wait_ge(we_lo_ready, DC)
            cond_y(0, 0, 1)
            pe.wait_ge(ad_at_ready, 1)
            pe.wait_ge(setup_evac, 2)
            for half in range(PER):
                pe.wait_ge(bd_in[half], 16 * (NT - 1))
            iteration(0, first=True)
            with pe.Fori(1, ITER_A) as i:
                iteration(i)
            def turn_down(n, par):
                pe.wait_ge(scaled, n + 1)
                wait(pe, wd_lo_ready, n - DOWN_U)
                for t in range(DC):
                    ins = pe.transpose(ps_t[:, t * P:(t + 1) * P], val[:, par, t * P:(t + 1) * P], ident[:, :])
                ins.then_inc(t_done, 1)

            adapter_ga(TAIL_U - 2, 0, CHUNKS - 1)
            ffn_z(NT - 2, 0)
            turn_unit(TAIL_U - 1, 2)
            adapter_bx(NT - 3)
            adapter_ga(TAIL_U - 1, 1, CHUNKS - 1)
            ffn_z(NT - 2, 1)
            turn_unit(TAIL_U, 0)
            cond_y(NT - 1, 1, NT // 2)
            adapter_ga(TAIL_U, 0, CHUNKS)
            turn_x1(NT - 2)
            pe.wait_ge(wt_ready, DOWN_U)
            turn_down(DOWN_U, 1)
            ffn_z(NT - 1, 0)
            adapter_bx(NT - 2)
            ffn_z(NT - 1, 1)
            turn_down(DOWN_U + 1, 0)
            turn_x1(NT - 1)
            adapter_bx(NT - 1)

            def gate_up(g, b, k):
                q = chunk_no(g, b, k)
                if b == 0:
                    loads = 1 if k == G else g + 1
                    pe.wait_ge(stage_in[k], 32 * loads)
                if not isinstance(g, int) or q >= G:
                    pe.wait_ge(silu_ready, q)
                    pe.wait_ge(inter_ready, q)
                cols = slice(b * HALF, (b + 1) * HALF)
                for m, ps in enumerate(gate_up_banks(g, b, k)):
                    for p, (w, v) in enumerate(((st_hi, bx_hi), (st_hi, bx_lo), (st_lo, bx_hi))):
                        ins = pe.matmul(ps, w[:, k, m, :], v[:, cols], start=p == 0, stop=p == 2)
                ins.then_inc(gu_mm, 1)

            def down(g, b, s, gpar):
                t = TPB * b + s
                if s == 0:
                    pe.wait_ge(in_lo_ready, chunk_no(g, b, G - 1) + 1)
                if s == 0 and b == 0:
                    pe.wait_ge(wd_lo_ready, G * (g + 1))
                wait(pe, added, NT * g + t - 1)
                for k in range(chunks_of(g)):
                    rows, wpar, wk = (REM, 1, 0) if k == G else (P, gpar, k)
                    if k == G and s == 0:
                        pe.wait_ge(in_lo_ready, chunk_no(g, b, k) + 1)
                        pe.wait_ge(wd_lo_ready, CHUNKS + 1)
                    for p, (v, vmore, w) in enumerate(((in_hi, wd_hi, wd_hi), (in_hi, wd_hi, wd_lo),
                                                       (in_lo, wd_lo, wd_hi))):
                        for h in range(2):
                            ins = pe.matmul(ps_o[t % 2][:, h * HALF:(h + 1) * HALF],
                                            half_slot(v, vmore, b, k, rows)[:, s * P:(s + 1) * P],
                                            w[0:rows, wpar, wk, h * HALF:(h + 1) * HALF],
                                            start=k == 0 and p == 0, stop=k == chunks_of(g) - 1 and p == 2)
                ins.then_inc(down_mm, 1)

            def group(g, gpar):
                n0 = DOWN_U + G * (g + 1)
                if is_last(g):
                    turn_down(DOWN_U + CHUNKS, 0)
                for b in range(NB):
                    before = next_unit(g, b - 1)
                    for s in range(TPB):
                        down(g, b, s, gpar)
                        work = next_chunk(g, b, s)
                        if work:
                            gate_up(*work)
                        if s == 1 and before is not None:
                            turn_down(n0 + before, par_of(gpar, before))

            pe.wait_ge(ga_evac, CHUNKS + 1)
            pe.wait_ge(bx_masked, NT)
            pe.wait_ge(bx_split, TPB)
            for k in range(G):
                gate_up(0, 0, k)
            turn_down(DOWN_U + 2, 1)
            pe.wait_ge(bx_split, NT)
            group(0, 0)
            group(1, 1)
            with pe.Fori(1, 2) as j:
                group(2 * j, 0)
                group(2 * j + 1, 1)
            for g in range(4, GROUPS):
                group(g, g % 2)


_INS = ["x", "itok_B_0_15", "itok_B_3_7", "L0_cond_weights", "L0_ffn_lora_A", "L0_ffn_lora_B", "L0_ffn_W",
        "L0_ffn_bias", "L0_ffn_lora_weights", "L1_cond_A", "L1_cond_B", "L1_ffn_gate_codes",
        "L1_ffn_gate_scales", "L1_ffn_up_codes", "L1_ffn_up_scales", "L1_ffn_down_codes", "L1_ffn_down_scales"]


def kernel(**inputs):
    import numpy as _np
    import concourse.bacc as _bacc
    from concourse import mybir as _mybir
    from concourse.bass_utils import run_bass_kernel_spmd as _run

    nc = _bacc.Bacc("TRN2", target_bir_lowering=False, num_devices=1)
    arrays, args = {}, []
    for name in _INS:
        a = _np.ascontiguousarray(inputs[name])
        arrays[f"in_{name}"] = a
        args.append(nc.dram_tensor(f"in_{name}", a.shape, _mybir.dt.from_np(a.dtype), kind="ExternalInput").ap())
    shape = inputs["x"].shape
    out = nc.dram_tensor("out", shape, _mybir.dt.float32, kind="ExternalOutput").ap()
    adaln_ffn(nc, *args, out)
    r = _run(nc, [arrays], core_ids=[0])
    return r.results[0]["out"]
```
